# Optimizing a Trainium2 kernel written in Bass

```python
import numpy as np
import jax
import jax.numpy as jnp

def _softmax(x, axis=-1):
    return jax.nn.softmax(x, axis=axis)

def _gelu(x):
    return jax.nn.gelu(x, approximate=True)

def _silu(x):
    return jax.nn.silu(x)

def _sigmoid(x):
    return jax.nn.sigmoid(x)

def _layernorm(x, axis=-1, eps=1e-05):
    m = jnp.mean(x, axis=axis, keepdims=True)
    v = jnp.var(x, axis=axis, keepdims=True)
    return (x - m) / jnp.sqrt(v + eps)

def _scatter_add(tgt, idx, src, axis=0):
    return tgt.at[idx].add(src)

def _segment_sum(src, seg, n):
    return jax.ops.segment_sum(src, seg, n)
kernel_name = 'mk_decoder_postln_d1_seqx_r8_e5a9b4'

def setup_inputs(seed: int=0):
    np.random.seed(seed)
    _w = jnp.asarray

    def _rec_inputs():
        import jax
        import jax.numpy as jnp
        _rk = jax.random.key(seed)
        x = -0.0002928 + 1 * jax.random.normal(jax.random.fold_in(_rk, 1), (8, 256, 128), jnp.float32)
        _lenS = 256 - jax.random.randint(jax.random.fold_in(_rk, 7), (8,), 0, max(1, 256 // 4) + 1, jnp.int32)
        _lenS2 = 64 - jax.random.randint(jax.random.fold_in(_rk, 8), (8,), 0, max(1, 64 // 4) + 1, jnp.int32)
        _ctx_1024P = jax.random.normal(jax.random.fold_in(_rk, 11), (8, 16, 128), jnp.float32)
        _ctx_1024c = jax.random.dirichlet(jax.random.fold_in(_rk, 511), 0.3 * jnp.ones((16,), jnp.float32), (8, 64))
        _ctx_1024t = jnp.einsum('bsk,bkd->bsd', _ctx_1024c, _ctx_1024P)
        _ctx_1024t = _ctx_1024t * jax.lax.rsqrt(jnp.mean(jnp.square(_ctx_1024t)) + 1e-12) * 0.953939
        ctx_1024 = 2.81802e-05 + 1.00001 * (_ctx_1024t + 0.3 * jax.random.normal(jax.random.fold_in(_rk, 611), (8, 64, 128), jnp.float32))
        return (x, ctx_1024)
    x, ctx_1024 = _rec_inputs()

    def _L0_attn_setup():
        import jax, jax.numpy as jnp
        import numpy as np
        D_MODEL = 128
        NUM_HEADS = 4
        HEAD_QK = 32
        HEAD_V = 64
        EPS = 1e-05
        ROPE_BASE = 10000.0

        def _apply_rotary(q, k):
            T, d = (q.shape[1], q.shape[-1])
            half = d // 2
            inv_freq = 1.0 / ROPE_BASE ** (jnp.arange(0, d, 2, dtype=jnp.float32) / d)
            freqs = jnp.arange(T, dtype=jnp.float32)[:, None] * inv_freq[None, :]
            cos = jnp.cos(freqs)[None, :, None, :]
            sin = jnp.sin(freqs)[None, :, None, :]

            def rot(x):
                x1, x2 = (x[..., :half], x[..., half:])
                return jnp.concatenate([x1 * cos - x2 * sin, x1 * sin + x2 * cos], axis=-1)
            return (rot(q), rot(k))
        key = jax.random.key(seed)
        ks = jax.random.split(key, 7)
        B, T = (2, 256)
        key_dim = NUM_HEADS * HEAD_QK
        value_dim = NUM_HEADS * HEAD_V
        s = 0.02
        return {'x': jax.random.normal(ks[0], (B, T, D_MODEL), jnp.float32), 'Wq': jax.random.normal(ks[1], (key_dim, D_MODEL), jnp.float32) * s, 'Wk': jax.random.normal(ks[2], (key_dim, D_MODEL), jnp.float32) * s, 'Wv': jax.random.normal(ks[3], (value_dim, D_MODEL), jnp.float32) * s, 'Wg': jax.random.normal(ks[4], (value_dim, D_MODEL), jnp.float32) * s, 'Wo': jax.random.normal(ks[5], (D_MODEL, value_dim), jnp.float32) * s, 'g_norm_w': jnp.ones((HEAD_V,), jnp.float32)}
    _L0_attn_all = _L0_attn_setup()
    _L0_attn_in = {k: v for k, v in _L0_attn_all.items() if k in ('Wq', 'Wk', 'Wv', 'Wg', 'Wo', 'g_norm_w')}
    del _L0_attn_all

    def _L0_xattn_setup():
        import jax, jax.numpy as jnp
        import numpy as np
        D_MODEL = 128
        N_HEADS = 16
        HEAD_DIM = D_MODEL // N_HEADS
        key = jax.random.key(seed)
        k1, k2, k3, k4, k5, k6 = jax.random.split(key, 6)
        B, T_q, T_kv = (4, 128, 512)
        s = 1.0 / np.sqrt(D_MODEL)
        return {'query': jax.random.normal(k1, (B, T_q, D_MODEL), dtype=jnp.float32), 'kv_source': jax.random.normal(k2, (B, T_kv, D_MODEL), dtype=jnp.float32), 'w_q': jax.random.normal(k3, (D_MODEL, D_MODEL), dtype=jnp.float32) * s, 'w_k': jax.random.normal(k4, (D_MODEL, D_MODEL), dtype=jnp.float32) * s, 'w_v': jax.random.normal(k5, (D_MODEL, D_MODEL), dtype=jnp.float32) * s, 'w_o': jax.random.normal(k6, (D_MODEL, D_MODEL), dtype=jnp.float32) * s}
    _L0_xattn_all = _L0_xattn_setup()
    _L0_xattn_in = {k: v for k, v in _L0_xattn_all.items() if k in ('w_q', 'w_k', 'w_v', 'w_o')}
    del _L0_xattn_all

    def _L0_ffn_setup():
        import jax, jax.numpy as jnp
        import numpy as np
        HIDDEN = 128
        NUM_EXPERTS = 8
        BATCH, SEQ = (4, 512)
        key = jax.random.key(seed)
        ks = jax.random.split(key, 6)
        s = 1.0 / np.sqrt(HIDDEN)
        tokens = jax.random.normal(ks[0], (BATCH, SEQ, HIDDEN), dtype=jnp.float32)
        gate_w = jax.random.uniform(ks[1], (NUM_EXPERTS, HIDDEN), jnp.float32, -s, s)
        expert_w = jax.random.uniform(ks[2], (NUM_EXPERTS, HIDDEN, HIDDEN), jnp.float32, -s, s)
        expert_b = jax.random.uniform(ks[3], (NUM_EXPERTS, HIDDEN), jnp.float32, -s, s)
        combine_w = jax.random.uniform(ks[4], (HIDDEN, HIDDEN), jnp.float32, -s, s)
        return {'tokens': tokens, 'gate_w': gate_w, 'expert_w': expert_w, 'expert_b': expert_b, 'combine_w': combine_w}
    _L0_ffn_all = _L0_ffn_setup()
    _L0_ffn_in = {k: v for k, v in _L0_ffn_all.items() if k in ('gate_w', 'expert_w', 'expert_b', 'combine_w')}
    del _L0_ffn_all
    return {'x': x, 'ctx_1024': ctx_1024, 'L0_attn_Wq': _L0_attn_in['Wq'], 'L0_attn_Wk': _L0_attn_in['Wk'], 'L0_attn_Wv': _L0_attn_in['Wv'], 'L0_attn_Wg': _L0_attn_in['Wg'], 'L0_attn_Wo': _L0_attn_in['Wo'], 'L0_attn_g_norm_w': _L0_attn_in['g_norm_w'], 'L0_xattn_w_q': _L0_xattn_in['w_q'], 'L0_xattn_w_k': _L0_xattn_in['w_k'], 'L0_xattn_w_v': _L0_xattn_in['w_v'], 'L0_xattn_w_o': _L0_xattn_in['w_o'], 'L0_ffn_gate_w': _L0_ffn_in['gate_w'], 'L0_ffn_expert_w': _L0_ffn_in['expert_w'], 'L0_ffn_expert_b': _L0_ffn_in['expert_b'], 'L0_ffn_combine_w': _L0_ffn_in['combine_w']}

def reference(x, ctx_1024, L0_attn_Wq, L0_attn_Wk, L0_attn_Wv, L0_attn_Wg, L0_attn_Wo, L0_attn_g_norm_w, L0_xattn_w_q, L0_xattn_w_k, L0_xattn_w_v, L0_xattn_w_o, L0_ffn_gate_w, L0_ffn_expert_w, L0_ffn_expert_b, L0_ffn_combine_w):
    import jax
    import jax.numpy as jnp

    def _L0_attn_ref(x, Wq, Wk, Wv, Wg, Wo, g_norm_w):
        import jax, jax.numpy as jnp
        import numpy as np
        D_MODEL = 128
        NUM_HEADS = 4
        HEAD_QK = 32
        HEAD_V = 64
        EPS = 1e-05
        ROPE_BASE = 10000.0

        def _apply_rotary(q, k):
            T, d = (q.shape[1], q.shape[-1])
            half = d // 2
            inv_freq = 1.0 / ROPE_BASE ** (jnp.arange(0, d, 2, dtype=jnp.float32) / d)
            freqs = jnp.arange(T, dtype=jnp.float32)[:, None] * inv_freq[None, :]
            cos = jnp.cos(freqs)[None, :, None, :]
            sin = jnp.sin(freqs)[None, :, None, :]

            def rot(x):
                x1, x2 = (x[..., :half], x[..., half:])
                return jnp.concatenate([x1 * cos - x2 * sin, x1 * sin + x2 * cos], axis=-1)
            return (rot(q), rot(k))
        B, T, _ = x.shape
        H, dk, dv = (NUM_HEADS, HEAD_QK, HEAD_V)
        q = (x @ Wq.T).reshape(B, T, H, dk)
        k = (x @ Wk.T).reshape(B, T, H, dk)
        q, k = _apply_rotary(q, k)
        q = jnp.transpose(q, (0, 2, 1, 3))
        k = jnp.transpose(k, (0, 2, 1, 3))
        v = jnp.transpose((x @ Wv.T).reshape(B, T, H, dv), (0, 2, 1, 3))
        q = q * dk ** (-0.5)
        log_decay = jnp.log1p(-jnp.exp2(-5.0 - jnp.arange(H, dtype=jnp.float32)))
        t = jnp.arange(T, dtype=jnp.float32)
        diff = t[:, None] - t[None, :]
        decay_mask = jnp.where(diff >= 0, jnp.exp(log_decay[:, None, None] * diff[None]), 0.0)
        scores = jnp.einsum('bhtd,bhsd->bhts', q, k) * decay_mask[None]
        o = jnp.einsum('bhts,bhsd->bhtd', scores, v)
        o = jnp.transpose(o, (0, 2, 1, 3))
        rms = jax.lax.rsqrt(jnp.mean(o * o, axis=-1, keepdims=True) + EPS)
        o_n = o * rms * g_norm_w
        g = (x @ Wg.T).reshape(B, T, H, dv)
        o_g = o_n * (g * jax.nn.sigmoid(g))
        return o_g.reshape(B, T, H * dv) @ Wo.T

    def _L0_xattn_ref(query, kv_source, w_q, w_k, w_v, w_o):
        import jax, jax.numpy as jnp
        import numpy as np
        D_MODEL = 128
        N_HEADS = 16
        HEAD_DIM = D_MODEL // N_HEADS
        B, T_q, _ = query.shape
        T_kv = kv_source.shape[1]
        q = (query @ w_q.T).reshape(B, T_q, N_HEADS, HEAD_DIM)
        k = (kv_source @ w_k.T).reshape(B, T_kv, N_HEADS, HEAD_DIM)
        v = (kv_source @ w_v.T).reshape(B, T_kv, N_HEADS, HEAD_DIM)
        scale = HEAD_DIM ** (-0.5)
        attn = jax.nn.softmax(jnp.einsum('bqhd,bkhd->bhqk', q, k) * scale, axis=-1)
        out = jnp.einsum('bhqk,bkhd->bqhd', attn, v).reshape(B, T_q, D_MODEL)
        return out @ w_o.T

    def _L0_ffn_ref(tokens, gate_w, expert_w, expert_b, combine_w):
        import jax, jax.numpy as jnp
        import numpy as np
        HIDDEN = 128
        NUM_EXPERTS = 8
        BATCH, SEQ = (4, 512)
        B, S, H = tokens.shape
        logits = jnp.einsum('bsh,eh->bse', tokens, gate_w)
        probs = jax.nn.softmax(logits, axis=-1)
        top2_w, top2_idx = jax.lax.top_k(probs, 2)
        flat = tokens.reshape(B * S, H)
        flat_idx = top2_idx.reshape(B * S, 2)
        flat_w = top2_w.reshape(B * S, 2)
        expert_out = jax.nn.silu(jnp.einsum('nh,edh->ned', flat, expert_w) + expert_b[None, :, :])
        gathered = jnp.take_along_axis(expert_out, flat_idx[:, :, None], axis=1)
        mixed = jnp.sum(gathered * flat_w[:, :, None], axis=1)
        out = jnp.einsum('bsh,dh->bsd', mixed.reshape(B, S, H), combine_w)
        return out
    x = _layernorm(x + _L0_attn_ref(x, L0_attn_Wq, L0_attn_Wk, L0_attn_Wv, L0_attn_Wg, L0_attn_Wo, L0_attn_g_norm_w), axis=-1)
    x = _layernorm(x + _L0_xattn_ref(x, ctx_1024, L0_xattn_w_q, L0_xattn_w_k, L0_xattn_w_v, L0_xattn_w_o), axis=-1)
    x = _layernorm(x + _L0_ffn_ref(x, L0_ffn_gate_w, L0_ffn_expert_w, L0_ffn_expert_b, L0_ffn_combine_w), axis=-1)
    return x

_drawn_inputs = setup_inputs


def setup_inputs(seed=0):
    import zlib

    import numpy as np

    out = dict(_drawn_inputs(seed))
    spreads = {'L0_attn_g_norm_w': (1.0, 0.6)}
    factors = {'L0_ffn_expert_b': 8.0}
    for name, (base, spread) in spreads.items():
        noise = np.random.default_rng([zlib.crc32(name.encode()), seed]).standard_normal(out[name].shape)
        drawn = base * np.exp(spread * noise) if base else spread * noise
        out[name] = jnp.asarray(drawn.astype(out[name].dtype))
    for name, factor in factors.items():
        out[name] = (out[name] * factor).astype(out[name].dtype)
    return out
```

```python
import concourse.bass as bass
from concourse import mybir
from contextlib import ExitStack

F32 = mybir.dt.float32
F32R = mybir.dt.float32r
BF16 = mybir.dt.bfloat16
U32 = mybir.dt.uint32
ALU = mybir.AluOpType
ACT = mybir.ActivationFunctionType
AX = mybir.AxisListType

B, T, D = 8, 256, 128
P = 128
J = T // P
RH, RV = 4, 64
RK = D // RH
XH, XK, XD = 16, 64, 8
PAIRS = XH // 2
VW = 2 * XD + 2
E = 8
EPS = 1e-5

EVENTS = """
qk_proj perm_proj v_proj g_proj rope_cos rope_sin qk_rotated v_kept gate_tanh gate_kept
ret_scores diag0_kept diag1_kept cross_kept ret_out squares_kept square_sums
rms_eps rms_rate gated gated_scaled gT_done gT_kept ret_proj
res1 stats1 moments1 var1_eps rate1 x1_tile0 x1_kept x1T_done x1T_kept
q_done q_kept
xs0 xs1 max0 max1 hi0 hi1 lo0 lo1 mT0 mT1 mT0_kept mT1_kept shifted0 shifted1 exp0 exp1
pT00 pT01 pT10 pT11 pT00_kept pT01_kept pT10_kept pT11_kept av0 av1
sums0_inv sums1_inv att0 att1 attT_done attT_kept x_proj
x2_held res2 stats2 moments2 var2_eps rate2 x2_tile0 x2_kept x2T_done x2T_kept x2T_held logits logits_kept
x2T_here w_here z0 z1 h0 h1 mixed0 mixed1 mixT_done mixT_kept comb
res3 stats3 moments3 var3_eps rate3 y_tile0 y_kept
""".split()
ONCE = """
xT_loaded x_loaded w_loaded w2_loaded tables_loaded ffn_loaded ctx_loaded out_stored
wo_scaled v_cleared kx_proj kx_kept vx_proj vx_kept kbd_made vbd_made const_made
bias_hi bias_lo top_max top_idx idx_float top_diff top_exp top_sum top_inv top_prob one_hot weighted w_ready
""".split()


def post_ln_decoder(nc, a, out):
    ctx = ExitStack()
    with ctx:
        def sb(name, shape, dt=F32):
            return ctx.enter_context(nc.sbuf_tensor(name, shape, dt))

        s = {n: ctx.enter_context(nc.semaphore(n)) for n in EVENTS + ONCE}
        mix = [[ctx.enter_context(nc.semaphore(f"mix{j}_{e}")) for e in range(E - 1)] for j in range(J)]

        w_rope = sb("w_rope", [D, 4, D])
        w_vg = sb("w_vg", [D, 2, RH * RV])
        w_ret_o = sb("w_ret_o", [P, 2, D])
        norm_w = sb("norm_w", [P, 1])
        w_x = sb("w_x", [D, 4, D])
        gate_w = sb("gate_w", [D, E])
        expert_w = sb("expert_w", [D, E * D])
        comb_w = sb("comb_w", [D, D])
        cos_t = sb("cos_t", [D, 2, T])
        sin_t = sb("sin_t", [D, 2, T])
        ident = sb("ident", [P, P])
        ident16 = sb("ident16", [P, P], BF16)
        causal = sb("causal", [P, P])
        head_mask = sb("head_mask", [P, XH])
        head_pick = sb("head_pick", [2 * XH, XH * XK])
        head_pick16 = sb("head_pick16", [2 * XH, XH * XK], BF16)
        iota_e = sb("iota_e", [P, E])
        ones_r = sb("ones_r", [64, P], F32R)
        bias_in = sb("bias_in", [64, E * D])
        bias_r = sb("bias_r", [64, E * D], F32R)
        ctxT = sb("ctxT", [D, B * XK])
        kT = sb("kT", [D, B * XK])
        k_bd = sb("k_bd", [D, B, XH, XK])
        v_bd = sb("v_bd", [P, B, PAIRS, VW])
        xT = sb("xT", [D, T])
        x_in = sb("x_in", [P, J, D])
        r_cos = sb("r_cos", [D, 2 * T])
        r_sin = sb("r_sin", [D, 2 * T])
        qk = sb("qk", [D, 2, T])
        v = sb("v", [P, J, RH * RV])
        g_tanh = sb("g_tanh", [P, J * RH * RV])
        gate = sb("gate", [P, J, RH * RV])
        p_diag = sb("p_diag", [P, J, RH, P])
        p_cross = sb("p_cross", [P, RH, P])
        squares = sb("squares", [P, J * RH, RV])
        ssq = sb("ssq", [P, J * RH])
        ssq_eps = sb("ssq_eps", [P, J * RH])
        rms = sb("rms", [P, J * RH])
        eps_ln = sb("eps_ln", [P, J])
        eps_sum = sb("eps_sum", [P, J * RH])
        minus_half = sb("minus_half", [P, J * RH])
        u = sb("u", [P, J * RH, RV])
        og = sb("og", [P, J, 2, P])
        ogT = sb("ogT", [P, J, 2, P])
        x1 = sb("x1", [P, J, D])
        x1T = sb("x1T", [D, T])
        ln = [dict(sum=sb(f"ln{n}_sum", [P, J, D]), stats=sb(f"ln{n}_stats", [P, J, 6]),
                              mv=sb(f"ln{n}_mv", [P, J, 2]), var=sb(f"ln{n}_var", [P, J]),
                              tick=sb(f"ln{n}_tick", [P, 1]), rate=sb(f"ln{n}_rate", [P, J])) for n in range(3)]
        qT = sb("qT", [D, T])
        neg_max = sb("neg_max", [P, J, XH])
        max16 = sb("max16", [P, J, 2 * XH], BF16)
        maxT = sb("maxT", [2 * XH, J, P], BF16)
        probs = sb("probs", [P, J, XH * XK])
        probsT = sb("probsT", [P, J, PAIRS, P])
        sums_inv = sb("sums_inv", [P, J, PAIRS, 2])
        att = sb("att", [P, J, D])
        attT = sb("attT", [D, T])
        x2 = sb("x2", [P, J, D])
        x2_all = sb("x2_all", [P, B, J, D])
        x2T = sb("x2T", [D, T])
        x2T_all = sb("x2T_all", [D, B, T])
        lg = sb("lg", [P, B * J, E])
        top = sb("top", [P, B * J, 8])
        top_at = sb("top_at", [P, B * J, 8], U32)
        top_atf = sb("top_atf", [P, B * J, 2])
        top_d = sb("top_d", [P, B * J, 8])
        top_e = sb("top_e", [P, B * J, 8])
        top_s = sb("top_s", [P, B * J])
        top_r = sb("top_r", [P, B * J])
        top_p = sb("top_p", [P, B * J, 2])
        hot = sb("hot", [P, B * J, 2, E])
        w_hot = sb("w_hot", [P, B * J, 2, E])
        w_all = sb("w_all", [P, B, J * E])
        w_now = sb("w_now", [P, J * E])
        x2T_now = sb("x2T_now", [D, T])
        h = sb("h", [P, J, E, D])
        acc = sb("acc", [P, J, E, D])
        mixT = sb("mixT", [D, T])
        y = sb("y", [P, J, D])

        bank = ctx.enter_context(nc.psum_tensor("bank", [P, 8, 512], F32))
        ret = bank[:, 0:4, :]
        X0, XA, XB = 4, 6, 7

        block = ctx.enter_context(nc.Block())

        @block.sync
        def _(sp):
            sp.dma_start(xT[:, :], a["xT"][:, 0:T]).then_inc(s["xT_loaded"], 16)
            sp.dma_start(w_rope[:, :, :], a["w_rope"]).then_inc(s["w_loaded"], 16)
            sp.dma_start(cos_t[:, :, :], a["cos_t"]).then_inc(s["tables_loaded"], 16)
            sp.dma_start(sin_t[:, :, :], a["sin_t"]).then_inc(s["tables_loaded"], 16)
            sp.dma_start(causal[:, :], a["causal"]).then_inc(s["tables_loaded"], 16)
            sp.dma_start(ctxT[:, :], a["ctxT"]).then_inc(s["ctx_loaded"], 16)
            sp.dma_start(head_mask[:, :], a["head_mask"]).then_inc(s["ctx_loaded"], 16)
            sp.dma_start(head_pick[:, :], a["head_pick"]).then_inc(s["ctx_loaded"], 16)
            sp.dma_start(x_in[:, :, :], a["x"][0]).then_inc(s["x_loaded"], 16)
            with sp.Fori(1, B) as b:
                sp.wait_ge(s["g_proj"], b)
                sp.dma_start(xT[:, :], a["xT"][:, bass.ds(b * T, T)]).then_inc(s["xT_loaded"], 16)
                sp.wait_ge(s["res1"], b)
                sp.dma_start(x_in[:, :, :], a["x"][bass.ds(b, 1)].rearrange("o p j d -> p (o j) d")).then_inc(s["x_loaded"], 16)
            with sp.Fori(0, B) as b:
                sp.wait_ge(s["y_kept"], b + 1)
                sp.dma_start(out[bass.ds(b, 1)].rearrange("o p j d -> p (o j) d"), y[:, :, :]).then_inc(s["out_stored"], 16)
            sp.wait_ge(s["out_stored"], 16 * B)

        @block.gpsimd
        def _(pool):
            pool.memset(v_bd[:, :, :, :], 0.0).then_inc(s["v_cleared"], 1)
            pool.memset(minus_half[:, :], -0.5)
            pool.memset(eps_ln[:, :], EPS)
            pool.memset(eps_sum[:, :], EPS * RV)
            pool.memset(ones_r[:, :].bitcast(F32), 1.0).then_inc(s["const_made"], 1)
            pool.wait_ge(s["ctx_loaded"], 48)
            pool.tensor_copy(head_pick16[:, :], head_pick[:, :]).then_inc(s["const_made"], 1)

            def power(var, var_eps, rate, eps, ready, eps_done, done, v_):
                n = var.shape[-1]
                pool.wait_ge(ready, v_)
                pool.tensor_tensor(var_eps, var, eps, ALU.add).then_inc(eps_done, 1)
                pool.wait_ge(eps_done, v_)
                pool.tensor_tensor(rate, var_eps, minus_half[:, 0:n], ALU.pow).then_inc(done, 1)

            def rms_power(b):
                power(ssq[:, :], ssq_eps[:, :], rms[:, :], eps_sum[:, :], s["square_sums"], s["rms_eps"], s["rms_rate"], b + 1)

            def norm1_power(b):
                power(ln[0]["mv"][:, :, 1], ln[0]["var"][:, :], ln[0]["rate"][:, :], eps_ln[:, :], s["moments1"], s["var1_eps"], s["rate1"], b + 1)

            def cross(b, v_):
                power(ln[1]["mv"][:, :, 1], ln[1]["var"][:, :], ln[1]["rate"][:, :], eps_ln[:, :], s["moments2"], s["var2_eps"], s["rate2"], v_)
                pool.wait_ge(s["x2_kept"], v_)
                pool.tensor_copy(x2_all[:, bass.ds(b, 1), :, :].rearrange("p o j d -> p (o j) d"), x2[:, :, :]).then_inc(s["x2_held"], 1)
                pool.wait_ge(s["x2T_kept"], v_)
                pool.tensor_copy(x2T_all[:, bass.ds(b, 1), :].rearrange("p o t -> p (o t)"), x2T[:, :]).then_inc(s["x2T_held"], 1)

            rms_power(0)
            norm1_power(0)
            with pool.Fori(1, B) as i:
                rms_power(i)
                cross(i - 1, i)
                norm1_power(i)
            cross(B - 1, B)

            pool.wait_ge(s["x2T_held"], B)
            pool.wait_ge(s["w_ready"], 1)
            with pool.Fori(0, B) as b:
                pool.wait_ge(s["z1"], b)
                pool.tensor_copy(x2T_now[:, :], x2T_all[:, bass.ds(b, 1), :].rearrange("p o t -> p (o t)")).then_inc(s["x2T_here"], 1)
                pool.wait_ge(s["mixed1"], b)
                pool.tensor_copy(w_now[:, :], w_all[:, bass.ds(b, 1), :].rearrange("p o t -> p (o t)")).then_inc(s["w_here"], 1)
                power(ln[2]["mv"][:, :, 1], ln[2]["var"][:, :], ln[2]["rate"][:, :], eps_ln[:, :], s["moments3"], s["var3_eps"], s["rate3"], b + 1)

        @block.scalar
        def _(act):
            act.dma_start(ident[:, :], a["ident"]).then_inc(s["w2_loaded"], 16)
            act.dma_start(w_vg[:, :, :], a["w_vg"]).then_inc(s["w2_loaded"], 16)
            act.dma_start(w_ret_o[:, :, :], a["w_ret_o"]).then_inc(s["w2_loaded"], 16)
            act.dma_start(norm_w[:, :], a["norm_w"]).then_inc(s["w2_loaded"], 16)
            act.dma_start(w_x[:, :, :], a["w_x"]).then_inc(s["w2_loaded"], 16)
            act.dma_start(gate_w[:, :], a["gate_w"]).then_inc(s["ffn_loaded"], 16)
            act.dma_start(expert_w[:, :], a["expert_w"]).then_inc(s["ffn_loaded"], 16)
            act.dma_start(comb_w[:, :], a["comb_w"]).then_inc(s["ffn_loaded"], 16)
            act.dma_start(iota_e[:, :], a["iota_e"]).then_inc(s["ffn_loaded"], 16)
            act.dma_start(bias_in[:, :], a["bias"]).then_inc(s["ffn_loaded"], 16)

            def retention_1(b):
                act.wait_ge(s["v_proj"], b + 1)
                act.wait_ge(s["ret_out"], b)
                act.activation(v[:, :, :], ret[:, 2, :].rearrange("p (j n) -> p j n", j=J), ACT.Copy).then_inc(s["v_kept"], 1)
                act.wait_ge(s["g_proj"], b + 1)
                act.wait_ge(s["gate_kept"], b)
                act.activation(g_tanh[:, :], ret[:, 3, :], ACT.Tanh, scale=0.5).then_inc(s["gate_tanh"], 1)

            def retention_2(b):
                act.wait_ge(s["ret_scores"], b + 1)
                act.wait_ge(s["ret_out"], b)
                act.activation(p_cross[:, :, :], ret[:, :, P:2 * P], ACT.Copy).then_inc(s["cross_kept"], 1)

            def retention_3(b):
                act.wait_ge(s["ret_out"], b + 1)
                act.wait_ge(s["square_sums"], b)
                act.activation(squares[:, :, :], ret[:, 0, :].rearrange("p (n c) -> p n c", c=RV), ACT.Square).then_inc(s["squares_kept"], 1)

            def retention_4(b):
                act.wait_ge(s["gT_done"], b + 1)
                act.wait_ge(s["ret_proj"], b)
                act.activation(ogT[:, :, :, :], ret[:, 1, :].rearrange("p (j n c) -> p j n c", j=J, n=2), ACT.Copy).then_inc(s["gT_kept"], 1)

            def retention_5(b):
                act.wait_ge(s["x1T_done"], b + 1)
                act.wait_ge(s["q_done"], b)
                act.activation(x1T[:, :], ret[:, 3, 0:T], ACT.Copy).then_inc(s["x1T_kept"], 1)

            def query(v_, p_):
                act.wait_ge(s["q_done"], v_)
                act.wait_ge(s["xs1"], p_)
                act.activation(qT[:, :], bank[:, XA, 0:T], ACT.Copy, scale=XD ** -0.5).then_inc(s["q_kept"], 1)

            def max_out(j, v_, p_):
                act.wait_ge((s["mT0"], s["mT1"])[j], v_)
                act.wait_ge((s["shifted0"], s["shifted1"])[j], p_)
                act.activation(maxT[:, j, :], bank[0:2 * XH, XB, 0:P // 2].bitcast(BF16), ACT.Copy).then_inc((s["mT0_kept"], s["mT1_kept"])[j], 1)

            def exponent(j, v_, p_):
                act.wait_ge((s["shifted0"], s["shifted1"])[j], v_)
                act.wait_ge((s["pT01"], s["pT11"])[j], p_)
                act.activation(probs[:, j, :], bank[:, X0:X0 + 2, :].rearrange("p n c -> p (n c)"), ACT.Exp).then_inc((s["exp0"], s["exp1"])[j], 1)

            def probs_out(j, half, v_, p_):
                act.wait_ge(((s["pT00"], s["pT01"]), (s["pT10"], s["pT11"]))[j][half], v_)
                act.wait_ge((s["av0"], s["av1"])[j], p_)
                act.activation(probsT[:, j, 4 * half:4 * half + 4, :],
                               bank[:, (XA, XB)[half], :].rearrange("p (n c) -> p n c", c=P), ACT.Copy)\
                   .then_inc(((s["pT00_kept"], s["pT01_kept"]), (s["pT10_kept"], s["pT11_kept"]))[j][half], 1)

            def att_out(v_, p_):
                act.wait_ge(s["attT_done"], v_)
                act.wait_ge(s["x_proj"], p_)
                act.activation(attT[:, :], bank[:, XB, 0:T], ACT.Copy).then_inc(s["attT_kept"], 1)

            def x2_out(b, v_, p_):
                act.wait_ge(s["x2T_done"], v_)
                act.wait_ge(s["logits"], p_)
                act.wait_ge(s["x2T_held"], p_)
                act.activation(x2T[:, :], bank[:, XB, 0:T], ACT.Copy).then_inc(s["x2T_kept"], 1)
                act.wait_ge(s["logits"], v_)
                act.activation(lg[:, bass.ds(b * J, J), :],
                               bank[:, XA, 0:J * E].rearrange("p (j e) -> p j e", j=J), ACT.Copy).then_inc(s["logits_kept"], 1)

            act.preload_act_table_set("exp_and_others")
            act.wait_ge(s["kx_proj"], 1)
            act.activation(kT[:, :], bank[:, X0, :], ACT.Copy).then_inc(s["kx_kept"], 1)
            for half in range(2):
                for b in range(B):
                    act.wait_ge(s["vx_proj"], half * B + b + 1)
                    if half == 0 and b == 0:
                        act.wait_ge(s["v_cleared"], 1)
                    lo = XK * half
                    act.activation(v_bd[lo:lo + XK, b, :, XD * half:XD * half + XD],
                                   bank[lo:lo + XK, XA + b % 2, 0:D].rearrange("p (n w c) -> p n w c", w=2, c=XD)[:, :, half, :],
                                   ACT.Copy).then_inc(s["vx_kept"], 1)

            retention_1(0)
            retention_2(0)
            retention_3(0)
            retention_4(0)
            retention_5(0)
            with act.Fori(1, B) as i:
                c, v_, p_ = i - 1, i, i - 1
                query(v_, p_)
                retention_1(i)
                max_out(0, v_, p_)
                exponent(0, v_, p_)
                retention_2(i)
                probs_out(0, 0, v_, p_)
                probs_out(0, 1, v_, p_)
                max_out(1, v_, p_)
                exponent(1, v_, p_)
                retention_3(i)
                probs_out(1, 0, v_, p_)
                probs_out(1, 1, v_, p_)
                retention_4(i)
                att_out(v_, p_)
                x2_out(c, v_, p_)
                retention_5(i)
            query(B, B - 1)
            for j in range(J):
                max_out(j, B, B - 1)
                exponent(j, B, B - 1)
                probs_out(j, 0, B, B - 1)
                probs_out(j, 1, B, B - 1)
            att_out(B, B - 1)
            x2_out(B - 1, B, B - 1)
            act.wait_ge(s["top_diff"], 1)
            act.activation(top_e[:, :, :], top_d[:, :, :], ACT.Exp).then_inc(s["top_exp"], 1)

            with act.Fori(0, B) as b:
                for j in range(J):
                    act.wait_ge((s["z0"], s["z1"])[j], b + 1)
                    act.wait_ge((s["mixed0"], s["mixed1"])[j], b)
                    act.activation(h[:, j, :, :], bank[:, 2 * j:2 * j + 2, :].rearrange("p n (e d) -> p (n e) d", d=D),
                                   ACT.Silu).then_inc((s["h0"], s["h1"])[j], 1)
                act.wait_ge(s["mixT_done"], b + 1)
                act.wait_ge(s["comb"], b)
                act.activation(mixT[:, :], bank[:, 4, 0:T], ACT.Copy).then_inc(s["mixT_kept"], 1)

        def layer_norm(dve, n, add_a, add_b, res, stats, moments, rate, tile0, kept, dst, v_, ready, free):
            t = ln[n]
            for sem, val in ready:
                dve.wait_ge(sem, val)
            dve.tensor_tensor(t["sum"][:, :, :], add_a, add_b, ALU.add).then_inc(res, 1)
            dve.wait_ge(res, v_)
            for j in range(J):
                last = dve.bn_stats(t["stats"][:, j, :], t["sum"][:, j, :])
            last.then_inc(stats, 1)
            dve.wait_ge(stats, v_)
            dve.memset(t["tick"][:, :], 0.0)
            for j in range(J):
                last = dve.bn_aggr(t["mv"][:, j, :], t["stats"][:, j, :])
            last.then_inc(moments, 1)
            dve.wait_ge(rate, v_)
            for sem, val in free:
                dve.wait_ge(sem, val)
            for j in range(J):
                dve.tensor_scalar(dst(j), t["sum"][:, j, :], t["mv"][:, j, 0:1], t["rate"][:, j:j + 1], ALU.subtract, ALU.mult)\
                   .then_inc((tile0, kept)[j], 1)

        @block.vector
        def _(dve):
            dve.wait_ge(s["w2_loaded"], 80)
            dve.wait_ge(s["const_made"], 1)
            dve.tensor_scalar(w_ret_o[:, :, :], w_ret_o[:, :, :], norm_w[:, 0:1], 0.5 * RV ** 0.5, ALU.mult, ALU.mult).then_inc(s["wo_scaled"], 1)
            dve.tensor_copy(ident16[:, :], ident[:, :]).then_inc(s["wo_scaled"], 1)

            def rope(b):
                dve.wait_ge(s["qk_proj"], b + 1)
                dve.wait_ge(s["qk_rotated"], b)
                dve.tensor_tensor(r_cos[:, :], ret[:, 0, :], cos_t[:, :, :].rearrange("p a t -> p (a t)"), ALU.mult).then_inc(s["rope_cos"], 1)
                dve.wait_ge(s["perm_proj"], b + 1)
                dve.tensor_tensor(r_sin[:, :], ret[:, 1, :], sin_t[:, :, :].rearrange("p a t -> p (a t)"), ALU.mult).then_inc(s["rope_sin"], 1)
                dve.wait_ge(s["rope_sin"], b + 1)
                dve.wait_ge(s["ret_scores"], b)
                dve.tensor_tensor(qk[:, :, :].rearrange("p a t -> p (a t)"), r_cos[:, :], r_sin[:, :], ALU.add).then_inc(s["qk_rotated"], 1)

            def gates(b):
                dve.wait_ge(s["gate_tanh"], b + 1)
                dve.wait_ge(s["gated"], b)
                dve.scalar_tensor_tensor(gate[:, :, :].rearrange("p j n -> p (j n)"), g_tanh[:, :], 1.0, ret[:, 3, :],
                                         ALU.add, ALU.mult).then_inc(s["gate_kept"], 1)

            def masks(b):
                dve.wait_ge(s["ret_scores"], b + 1)
                dve.wait_ge(s["ret_out"], b)
                dve.wait_ge(s["cross_kept"], b + 1)
                m = causal[:, :].unsqueeze(1).broadcast_to([P, RH, P])
                dve.tensor_tensor(p_diag[:, 0, :, :], ret[:, :, 0:P], m, ALU.mult).then_inc(s["diag0_kept"], 1)
                dve.tensor_tensor(p_diag[:, 1, :, :], ret[:, :, 2 * P:3 * P], m, ALU.mult).then_inc(s["diag1_kept"], 1)

            def sums(b):
                dve.wait_ge(s["squares_kept"], b + 1)
                dve.tensor_tensor(u[:, :, :], gate[:, :, :].rearrange("p j (n c) -> p (j n) c", c=RV),
                                  ret[:, 0, :].rearrange("p (n c) -> p n c", c=RV), ALU.mult).then_inc(s["gated"], 1)
                dve.tensor_reduce(ssq[:, :], squares[:, :, :], AX.X, ALU.add).then_inc(s["square_sums"], 1)

            def scale_rms(b):
                dve.wait_ge(s["rms_rate"], b + 1)
                dve.wait_ge(s["gT_done"], b)
                dve.tensor_tensor(og[:, :, :, :].rearrange("p j n (m c) -> p (j n m) c", c=RV), u[:, :, :],
                                  rms[:, :].unsqueeze(2).broadcast_to([P, J * RH, RV]), ALU.mult).then_inc(s["gated_scaled"], 1)

            def norm1(b, x2_value):
                layer_norm(dve, 0, ret[:, 2, 0:T].rearrange("p (j d) -> p j d", j=J), x_in[:, :, :],
                           s["res1"], s["stats1"], s["moments1"], s["rate1"], s["x1_tile0"], s["x1_kept"], lambda j: x1[:, j, :], b + 1,
                           [(s["ret_proj"], b + 1), (s["x_loaded"], 16 * (b + 1)), (s["x1_kept"], b)], [(s["res2"], x2_value), (s["x1T_done"], b)])

            def maxima(j, v_, p_):
                dve.wait_ge((s["xs0"], s["xs1"])[j], v_)
                sc = bank[:, X0:X0 + 2, :].rearrange("p n (h k) -> p (n h) k", k=XK)
                dve.tensor_reduce(neg_max[:, j, :], sc, AX.X, ALU.max, negate=True).then_inc((s["max0"], s["max1"])[j], 1)
                dve.wait_ge((s["max0"], s["max1"])[j], v_)
                dve.wait_ge((s["mT0"], s["mT1"])[j], p_)
                dve.tensor_copy(max16[:, j, 0:XH], neg_max[:, j, :]).then_inc((s["hi0"], s["hi1"])[j], 1)
                dve.wait_ge((s["hi0"], s["hi1"])[j], v_)
                dve.tensor_tensor(max16[:, j, XH:2 * XH], neg_max[:, j, :], max16[:, j, 0:XH], ALU.subtract)\
                   .then_inc((s["lo0"], s["lo1"])[j], 1)

            def attended(j, v_, p_):
                dve.wait_ge((s["av0"], s["av1"])[j], v_)
                av = bank[:, XA, 0:PAIRS * VW].rearrange("p (n c) -> p n c", c=VW)
                dve.reciprocal(sums_inv[:, j, :, :], av[:, :, 2 * XD:VW]).then_inc((s["sums0_inv"], s["sums1_inv"])[j], 1)
                dve.wait_ge((s["sums0_inv"], s["sums1_inv"])[j], v_)
                dve.wait_ge(s["attT_done"], p_)
                dve.tensor_tensor(att[:, j, :].rearrange("p (n w c) -> p n w c", w=2, c=XD),
                                  av[:, :, 0:2 * XD].rearrange("p n (w c) -> p n w c", c=XD),
                                  sums_inv[:, j, :, :].unsqueeze(3).broadcast_to([P, PAIRS, 2, XD]), ALU.mult)\
                   .then_inc((s["att0"], s["att1"])[j], 1)

            def norm2(b, v_, p_):
                layer_norm(dve, 1, bank[:, XA, 0:T].rearrange("p (j d) -> p j d", j=J), x1[:, :, :],
                           s["res2"], s["stats2"], s["moments2"], s["rate2"], s["x2_tile0"], s["x2_kept"],
                           lambda j: x2[:, j, :], v_,
                           [(s["x_proj"], v_), (s["x2_kept"], p_)], [(s["x2T_done"], p_), (s["x2_held"], p_)])

            def block_keys(b):
                dve.tensor_tensor(k_bd[:, b, :, :], kT[:, b * XK:(b + 1) * XK].unsqueeze(1).broadcast_to([P, XH, XK]),
                                  head_mask[:, :].unsqueeze(2).broadcast_to([P, XH, XK]), ALU.mult).then_inc(s["kbd_made"], 1)

            dve.wait_ge(s["v_cleared"], 1)
            for half in range(2):
                dve.memset(v_bd[XK * half:XK * half + XK, :, :, 2 * XD + half:2 * XD + half + 1], 1.0).then_inc(s["vbd_made"], 1)
            dve.wait_ge(s["tables_loaded"], 48)
            rope(0)
            gates(0)
            masks(0)
            sums(0)
            scale_rms(0)
            dve.wait_ge(s["kx_kept"], 1)
            dve.wait_ge(s["ctx_loaded"], 48)
            for b in range(B):
                block_keys(b)
            norm1(0, 0)
            dve.wait_ge(s["ffn_loaded"], 80)
            dve.tensor_copy(bias_r[:, :], bias_in[:, :]).then_inc(s["bias_hi"], 1)
            dve.wait_ge(s["bias_hi"], 1)
            dve.tensor_tensor(bias_r[32:64, :], bias_in[32:64, :], bias_r[32:64, :].bitcast(F32), ALU.subtract).then_inc(s["bias_lo"], 1)
            with dve.Fori(1, B) as i:
                c, v_, p_ = i - 1, i, i - 1
                rope(i)
                maxima(0, v_, p_)
                gates(i)
                masks(i)
                maxima(1, v_, p_)
                attended(0, v_, p_)
                sums(i)
                scale_rms(i)
                attended(1, v_, p_)
                norm2(c, v_, p_)
                norm1(i, v_)
            for j in range(J):
                maxima(j, B, B - 1)
                attended(j, B, B - 1)
            norm2(B - 1, B, B - 1)

            dve.wait_ge(s["logits_kept"], B)
            for t in range(B * J):
                last = dve.max(top[:, t, :], lg[:, t, :])
            last.then_inc(s["top_max"], 1)
            dve.wait_ge(s["top_max"], 1)
            dve.tensor_tensor(top_d[:, :, :], top[:, :, :], top[:, :, 0:1].broadcast_to([P, B * J, 8]), ALU.subtract).then_inc(s["top_diff"], 1)
            for t in range(B * J):
                last = dve.max_index(top_at[:, t, :], top[:, t, :], lg[:, t, :])
            last.then_inc(s["top_idx"], 1)
            dve.wait_ge(s["top_idx"], 1)
            dve.tensor_copy(top_atf[:, :, :], top_at[:, :, 0:2]).then_inc(s["idx_float"], 1)
            dve.wait_ge(s["top_exp"], 1)
            dve.tensor_reduce(top_s[:, :], top_e[:, :, :], AX.X, ALU.add).then_inc(s["top_sum"], 1)
            dve.wait_ge(s["top_sum"], 1)
            dve.reciprocal(top_r[:, :], top_s[:, :]).then_inc(s["top_inv"], 1)
            dve.wait_ge(s["top_inv"], 1)
            dve.wait_ge(s["ffn_loaded"], 80)
            dve.tensor_tensor(top_p[:, :, :], top_e[:, :, 0:2], top_r[:, :].unsqueeze(2).broadcast_to([P, B * J, 2]), ALU.mult).then_inc(s["top_prob"], 1)
            for k in range(2):
                last = dve.tensor_tensor(hot[:, :, k, :], iota_e[:, :].unsqueeze(1).broadcast_to([P, B * J, E]),
                                         top_atf[:, :, k:k + 1].broadcast_to([P, B * J, E]), ALU.is_equal)
            last.then_inc(s["one_hot"], 1)
            dve.wait_ge(s["one_hot"], 1)
            dve.wait_ge(s["top_prob"], 1)
            for k in range(2):
                last = dve.tensor_tensor(w_hot[:, :, k, :], hot[:, :, k, :], top_p[:, :, k:k + 1].broadcast_to([P, B * J, E]), ALU.mult)
            last.then_inc(s["weighted"], 1)
            dve.wait_ge(s["weighted"], 1)
            dve.tensor_tensor(w_all[:, :, :].rearrange("p b (j e) -> p (b j) e", e=E), w_hot[:, :, 0, :], w_hot[:, :, 1, :], ALU.add).then_inc(s["w_ready"], 1)

            with dve.Fori(0, B) as b:
                dve.wait_ge(s["w_here"], b + 1)
                for j in range(J):
                    dve.wait_ge((s["h0"], s["h1"])[j], b + 1)
                    if j == 0:
                        dve.wait_ge(s["mixT_done"], b)
                for e in range(E):
                    for j in range(J):
                        w = w_now[:, j * E + e:j * E + e + 1]
                        if e == 0:
                            dve.tensor_scalar(acc[:, j, 0, :], h[:, j, 0, :], w, None, ALU.mult).then_inc(mix[j][0], 1)
                        else:
                            dve.wait_ge(mix[j][e - 1], b + 1)
                            dve.scalar_tensor_tensor(acc[:, j, e, :], h[:, j, e, :], w, acc[:, j, e - 1, :], ALU.mult, ALU.add)\
                               .then_inc(mix[j][e] if e < E - 1 else (s["mixed0"], s["mixed1"])[j], 1)
                layer_norm(dve, 2, bank[:, 5, 0:T].rearrange("p (j d) -> p j d", j=J),
                           x2_all[:, bass.ds(b, 1), :, :].rearrange("p o j d -> p (o j) d"),
                           s["res3"], s["stats3"], s["moments3"], s["rate3"], s["y_tile0"], s["y_kept"], lambda j: y[:, j, :], b + 1,
                           [(s["comb"], b + 1), (s["y_kept"], b)], [(s["out_stored"], 16 * b)])

        @block.tensor
        def _(pe):
            def mm(o, l, r, start=True, stop=True, **k):
                return pe.matmul(o, l, r, start=start, stop=stop, **k)

            def project(b, b16):
                pe.wait_ge(s["xT_loaded"], b16)
                pe.wait_ge(s["gated"], b)
                pe.wait_ge(s["squares_kept"], b)
                for n in range(2):
                    last = mm(ret[:, 0, n * T:(n + 1) * T], w_rope[:, n, :], xT[:, :])
                last.then_inc(s["qk_proj"], 1)
                pe.wait_ge(s["gT_kept"], b)
                for n in range(2):
                    last = mm(ret[:, 1, n * T:(n + 1) * T], w_rope[:, 2 + n, :], xT[:, :])
                last.then_inc(s["perm_proj"], 1)
                pe.wait_ge(s["res1"], b)
                for j in range(J):
                    last = mm(ret[:, 2, j * 256:(j + 1) * 256], xT[:, j * P:(j + 1) * P], w_vg[:, 0, :])
                last.then_inc(s["v_proj"], 1)
                pe.wait_ge(s["x1T_kept"], b)
                for j in range(J):
                    last = mm(ret[:, 3, j * 256:(j + 1) * 256], xT[:, j * P:(j + 1) * P], w_vg[:, 1, :])
                last.then_inc(s["g_proj"], 1)

            def ret_scores(b):
                pe.wait_ge(s["qk_rotated"], b + 1)
                pe.wait_ge(s["v_kept"], b + 1)
                pe.wait_ge(s["gate_kept"], b + 1)
                for blk, (sc, tq) in enumerate(((0, 0), (0, 1), (1, 1))):
                    for n in range(RH):
                        r = slice(RK * n, RK * n + RK)
                        last = mm(ret[:, n, blk * P:(blk + 1) * P], qk[r, 1, sc * P:(sc + 1) * P], qk[r, 0, tq * P:(tq + 1) * P],
                                  tile_position=(RK * n, 0))
                last.then_inc(s["ret_scores"], 1)

            def ret_out(b):
                pe.wait_ge(s["diag0_kept"], b + 1)
                pe.wait_ge(s["diag1_kept"], b + 1)
                pe.wait_ge(s["cross_kept"], b + 1)
                for n in range(RH):
                    o = ret[:, 0, n * RV:(n + 1) * RV]
                    vn = slice(n * RV, (n + 1) * RV)
                    mm(o, p_diag[:, 0, n, :], v[:, 0, vn])
                    o = ret[:, 0, 256 + n * RV:256 + (n + 1) * RV]
                    mm(o, p_cross[:, n, :], v[:, 0, vn], stop=False)
                    last = mm(o, p_diag[:, 1, n, :], v[:, 1, vn], start=False)
                last.then_inc(s["ret_out"], 1)

            def gT(b):
                pe.wait_ge(s["gated_scaled"], b + 1)
                for j in range(J):
                    for n in range(2):
                        k = 2 * j + n
                        last = pe.transpose(ret[:, 1, k * P:(k + 1) * P], og[:, j, n, :], ident[:, :])
                last.then_inc(s["gT_done"], 1)

            def ret_proj(b):
                pe.wait_ge(s["gT_kept"], b + 1)
                for j in range(J):
                    for n in range(2):
                        last = mm(ret[:, 2, j * P:(j + 1) * P], ogT[:, j, n, :], w_ret_o[:, n, :], start=n == 0, stop=n == 1)
                last.then_inc(s["ret_proj"], 1)

            def x1_T(b):
                pe.wait_ge(s["x1_kept"], b + 1)
                for j in range(J):
                    last = pe.transpose(ret[:, 3, j * P:(j + 1) * P], x1[:, j, :], ident[:, :])
                last.then_inc(s["x1T_done"], 1)

            def query(v_, p_):
                pe.wait_ge(s["x1T_kept"], v_)
                pe.wait_ge(s["logits_kept"], p_)
                mm(bank[:, XA, 0:T], w_x[:, 0, :], x1T[:, :]).then_inc(s["q_done"], 1)

            def scores(b, j, v_, p_):
                if j == 0:
                    pe.wait_ge(s["q_kept"], v_)
                    pe.wait_ge(s["exp1"], p_)
                else:
                    pe.wait_ge(s["exp0"], v_)
                kb = k_bd[:, bass.ds(b, 1), :, :].rearrange("p o (n h) k -> p (o n) (h k)", n=2)
                for n in range(2):
                    last = mm(bank[:, X0 + n, :], qT[:, j * P:(j + 1) * P], kb[:, n, :], skip_group_check=True)
                last.then_inc((s["xs0"], s["xs1"])[j], 1)

            def shift(j, v_, p_):
                pe.wait_ge((s["lo0"], s["lo1"])[j], v_)
                if j == 0:
                    pe.wait_ge(s["x2T_kept"], p_)
                else:
                    pe.wait_ge(s["pT01_kept"], v_)
                pe.transpose(bank[0:2 * XH, XB, 0:P // 2].bitcast(BF16), max16[:, j, :], ident16[:, :]).then_inc((s["mT0"], s["mT1"])[j], 1)
                pe.wait_ge((s["mT0_kept"], s["mT1_kept"])[j], v_)
                for n in range(2):
                    last = mm(bank[:, X0 + n, :], maxT[:, j, :], head_pick16[:, n * 512:(n + 1) * 512], start=False, skip_group_check=True)
                last.then_inc((s["shifted0"], s["shifted1"])[j], 1)

            def probs_T(j, v_, p_):
                pe.wait_ge((s["exp0"], s["exp1"])[j], v_)
                if j == 0:
                    pe.wait_ge(s["q_kept"], v_)
                else:
                    pe.wait_ge(s["att0"], v_)
                for half in range(2):
                    for n in range(4):
                        at = (4 * half + n) * P
                        last = pe.transpose(bank[:, (XA, XB)[half], n * P:(n + 1) * P], probs[:, j, at:at + P], ident[:, :])
                    last.then_inc(((s["pT00"], s["pT01"]), (s["pT10"], s["pT11"]))[j][half], 1)

            def values(b, j, v_):
                pe.wait_ge(((s["pT00_kept"]), (s["pT10_kept"]))[j], v_)
                pe.wait_ge(((s["pT01_kept"]), (s["pT11_kept"]))[j], v_)
                for n in range(PAIRS):
                    last = mm(bank[:, XA, n * VW:(n + 1) * VW], probsT[:, j, n, :],
                              v_bd[:, bass.ds(b, 1), n, :].rearrange("p o c -> p (o c)"))
                last.then_inc((s["av0"], s["av1"])[j], 1)

            def att_T(v_):
                pe.wait_ge(s["att0"], v_)
                pe.wait_ge(s["att1"], v_)
                pe.wait_ge(s["pT11_kept"], v_)
                for j in range(J):
                    last = pe.transpose(bank[:, XB, j * P:(j + 1) * P], att[:, j, :], ident[:, :])
                last.then_inc(s["attT_done"], 1)

            def x_proj(v_):
                pe.wait_ge(s["attT_kept"], v_)
                for j in range(J):
                    last = mm(bank[:, XA, j * P:(j + 1) * P], attT[:, j * P:(j + 1) * P], w_x[:, 3, :])
                last.then_inc(s["x_proj"], 1)

            def x2_T(b, v_):
                pe.wait_ge(s["x2_tile0"], v_)
                pe.wait_ge(s["x2_kept"], v_)
                for j in range(J):
                    last = pe.transpose(bank[:, XB, j * P:(j + 1) * P], x2[:, j, :], ident[:, :])
                last.then_inc(s["x2T_done"], 1)
                pe.wait_ge(s["x2T_kept"], v_)
                for j in range(J):
                    last = mm(bank[:, XA, j * E:(j + 1) * E], x2T[:, j * P:(j + 1) * P], gate_w[:, :])
                last.then_inc(s["logits"], 1)

            pe.wait_ge(s["w_loaded"], 16)
            pe.wait_ge(s["w2_loaded"], 80)
            project(0, 16)
            pe.wait_ge(s["ctx_loaded"], 48)
            mm(bank[:, X0, :], w_x[:, 1, :], ctxT[:, :]).then_inc(s["kx_proj"], 1)
            for half in range(2):
                for b in range(B):
                    n = half * B + b
                    if n >= 2:
                        pe.wait_ge(s["vx_kept"], n - 1)
                    mm(bank[XK * half:XK * half + XK, XA + b % 2, 0:D], ctxT[:, b * XK:(b + 1) * XK], w_x[:, 2, :],
                       tile_position=(0, XK * half)).then_inc(s["vx_proj"], 1)
            pe.wait_ge(s["wo_scaled"], 2)
            ret_scores(0)
            ret_out(0)
            gT(0)
            ret_proj(0)
            x1_T(0)
            pe.wait_ge(s["kx_kept"], 1)
            pe.wait_ge(s["vx_kept"], 2 * B)
            pe.wait_ge(s["vbd_made"], 2)
            pe.wait_ge(s["kbd_made"], B)
            pe.wait_ge(s["const_made"], 2)
            pe.wait_ge(s["ffn_loaded"], 80)
            with pe.Fori(1, B) as i:
                c, v_, p_ = i - 1, i, i - 1
                query(v_, p_)
                project(i, 16 * i + 16)
                scores(c, 0, v_, p_)
                shift(0, v_, p_)
                ret_scores(i)
                probs_T(0, v_, p_)
                scores(c, 1, v_, p_)
                values(c, 0, v_)
                ret_out(i)
                shift(1, v_, p_)
                probs_T(1, v_, p_)
                values(c, 1, v_)
                gT(i)
                att_T(v_)
                ret_proj(i)
                x_proj(v_)
                x2_T(c, v_)
                x1_T(i)
            query(B, B - 1)
            for j in range(J):
                scores(B - 1, j, B, B - 1)
                shift(j, B, B - 1)
                probs_T(j, B, B - 1)
                values(B - 1, j, B)
            att_T(B)
            x_proj(B)
            x2_T(B - 1, B)

            pe.wait_ge(s["bias_lo"], 1)
            pe.wait_ge(s["logits_kept"], B)
            with pe.Fori(0, B) as b:
                pe.wait_ge(s["x2T_here"], b + 1)
                for j in range(J):
                    pe.wait_ge((s["h0"], s["h1"])[j], b)
                    for n in range(2):
                        o = bank[:, 2 * j + n, :]
                        cols = slice(n * 512, (n + 1) * 512)
                        mm(o, x2T_now[:, j * P:(j + 1) * P], expert_w[:, cols], stop=False)
                        last = mm(o, ones_r[:, :], bias_r[:, cols], start=False)
                    last.then_inc((s["z0"], s["z1"])[j], 1)
                pe.wait_ge(s["mixed0"], b + 1)
                pe.wait_ge(s["mixed1"], b + 1)
                pe.wait_ge(s["mixT_kept"], b)
                for j in range(J):
                    last = pe.transpose(bank[:, 4, j * P:(j + 1) * P], acc[:, j, E - 1, :], ident[:, :])
                last.then_inc(s["mixT_done"], 1)
                pe.wait_ge(s["mixT_kept"], b + 1)
                pe.wait_ge(s["res3"], b)
                for j in range(J):
                    last = mm(bank[:, 5, j * P:(j + 1) * P], mixT[:, j * P:(j + 1) * P], comb_w[:, :])
                last.then_inc(s["comb"], 1)


def constants():
    import numpy as np
    half = RK // 2
    inv_freq = (1.0 / np.float32(10000.0) ** (np.arange(0, RK, 2, dtype=np.float32) / np.float32(RK))).astype(np.float32)
    angle = (np.arange(T, dtype=np.float32)[None, :] * inv_freq[:, None]).astype(np.float64)
    cos, sin = np.cos(angle), np.sin(angle)
    log_decay = np.log1p(-np.exp2(-5.0 - np.arange(RH)))[:, None, None] * np.arange(T)[None, None, :]
    cos_h = np.broadcast_to(np.concatenate([cos, cos])[None], (RH, RK, T))
    sin_h = np.broadcast_to(np.concatenate([-sin, sin])[None], (RH, RK, T))
    up, down = np.exp(log_decay) * RK ** -0.5, np.exp(-log_decay)
    c = {}
    c["cos_t"] = np.stack([cos_h * up, cos_h * down], axis=2).reshape(D, 2, T).astype(np.float32)
    c["sin_t"] = np.stack([sin_h * up, sin_h * down], axis=2).reshape(D, 2, T).astype(np.float32)
    c["causal"] = (np.arange(P)[:, None] <= np.arange(P)[None, :]).astype(np.float32)
    c["ident"] = np.eye(P, dtype=np.float32)
    c["head_mask"] = (np.arange(P)[:, None] // XD == np.arange(XH)[None, :]).astype(np.float32)
    c["head_pick"] = (np.arange(2 * XH)[:, None] % XH == np.arange(XH * XK)[None, :] // XK).astype(np.float32)
    c["iota_e"] = np.broadcast_to(np.arange(E, dtype=np.float32), (P, E)).copy()
    return c


def kernel(x, ctx_1024, L0_attn_Wq, L0_attn_Wk, L0_attn_Wv, L0_attn_Wg, L0_attn_Wo, L0_attn_g_norm_w,
           L0_xattn_w_q, L0_xattn_w_k, L0_xattn_w_v, L0_xattn_w_o,
           L0_ffn_gate_w, L0_ffn_expert_w, L0_ffn_expert_b, L0_ffn_combine_w):
    import numpy as np
    import concourse.bacc as bacc
    from concourse.bass_utils import run_bass_kernel_spmd

    def swap(w):
        return np.asarray(w).reshape(RH, 2, RK // 2, D)[:, ::-1].reshape(D, D)

    x = np.asarray(x)
    wq, wk = np.asarray(L0_attn_Wq), np.asarray(L0_attn_Wk)
    bias = np.zeros((64, E * D), np.float32)
    bias[0] = bias[32] = np.asarray(L0_ffn_expert_b).reshape(-1)
    arrays = constants()
    arrays["xT"] = x.reshape(B * T, D).T
    arrays["x"] = x.reshape(B, J, P, D).transpose(0, 2, 1, 3)
    arrays["w_rope"] = np.stack([wq.T, wk.T, swap(wq).T, swap(wk).T], axis=1)
    arrays["w_vg"] = np.stack([np.asarray(L0_attn_Wv).T, np.asarray(L0_attn_Wg).T], axis=1)
    arrays["w_ret_o"] = np.asarray(L0_attn_Wo).T.reshape(2, P, D).transpose(1, 0, 2)
    arrays["norm_w"] = np.tile(np.asarray(L0_attn_g_norm_w), P // RV).reshape(P, 1)
    arrays["w_x"] = np.stack([np.asarray(w).T for w in (L0_xattn_w_q, L0_xattn_w_k, L0_xattn_w_v, L0_xattn_w_o)], axis=1)
    arrays["ctxT"] = np.asarray(ctx_1024).reshape(B * XK, D).T
    arrays["gate_w"] = np.asarray(L0_ffn_gate_w).T
    arrays["expert_w"] = np.asarray(L0_ffn_expert_w).transpose(2, 0, 1).reshape(D, E * D)
    arrays["bias"] = bias
    arrays["comb_w"] = np.asarray(L0_ffn_combine_w).T
    arrays = {n: np.ascontiguousarray(v) for n, v in arrays.items()}

    nc = bacc.Bacc("TRN2", target_bir_lowering=False, num_devices=1)
    ins = {n: nc.dram_tensor(n + "_dram", v.shape, mybir.dt.from_np(v.dtype), kind="ExternalInput").ap() for n, v in arrays.items()}
    out = nc.dram_tensor("out_dram", (B, P, J, D), F32, kind="ExternalOutput").ap()
    post_ln_decoder(nc, ins, out)
    r = run_bass_kernel_spmd(nc, [{n + "_dram": v for n, v in arrays.items()}], core_ids=[0])
    return r.results[0]["out_dram"].transpose(0, 2, 1, 3).reshape(B, T, D)
```

```python
import concourse.bass as bass
from concourse import mybir
from contextlib import ExitStack

F32 = mybir.dt.float32
F32R = mybir.dt.float32r
BF16 = mybir.dt.bfloat16
U32 = mybir.dt.uint32
ALU = mybir.AluOpType
ACT = mybir.ActivationFunctionType
AX = mybir.AxisListType

B, T, D = 8, 256, 128
P = 128
J = T // P
RH, RV = 4, 64
RK = D // RH
VD = RH * RV
XH, XK, XD = 16, 64, 8
PAIRS = XH // 2
XG = 4
GH, GR = XH // XG, D // XG
VW = 2 * XD
E = 8
EPS = 1e-5
STAGES = 5

EVENTS = """
x_hi x_lo qk_proj v_proj g_proj rope_cos rope_sin rope_swap rotated k_spread v_kept gate_tanh gate_kept
score0 scorex score1 diag0 cross diag1
ret_out squares gated square_sums rms_eps rms_rate scaled gT gT_kept ret_proj
res1 stats1 moments1 var1_eps rate1 x1_kept x1_held x1T x1T_kept q_proj q_hi q_lo
q_picked q_spread k_masked max_scores0 max_scores1 max0 max1 max_hi max_lo maxT maxT_kept
scoresT0 scoresT1 exp0 exp1 v_placed av inv att x_proj
res2 stats2 moments2 var2_eps rate2 x2_kept x2_held x2T x2T_kept x2T_held logits logits_kept
top_max top_found top_exp top_sum top_inv top_prob weighted w_kept
y_here y_hi y_lo w_here z0 z1 h0 h1 mixed0 mixed1 mixT mixT_kept comb
res3 stats3 moments3 var3_eps rate3 mean3 shift3 y_kept
""".split()
ONCE = """
xT_loaded x_loaded rope_w_loaded vg_w_loaded tables_loaded ident_loaded out_w_loaded x_w_loaded ctx_loaded pick_loaded picks_made
ffn_loaded out_stored zeros_made consts_made
rope_w_hi vg_w_hi weights_made k_proj k_hi k_lo vx_proj vx_kept v_ones
expert_hi bias_lo
""".split()


def wait(engine, sem, value):
    if not isinstance(value, int) or value > 0:
        engine.wait_ge(sem, value)


def post_ln_decoder(nc, a, out):
    ctx = ExitStack()
    with ctx:
        def sb(name, shape, dt=F32):
            return ctx.enter_context(nc.sbuf_tensor(name, shape, dt))

        s = {n: ctx.enter_context(nc.semaphore(n)) for n in EVENTS + ONCE}
        mix_done = [[ctx.enter_context(nc.semaphore(f"mix{j}_{e}")) for e in range(E - 1)] for j in range(J)]

        w_qk = sb("w_qk", [D, 2, D])
        w_qk_r = sb("w_qk_r", [D, 2, 2, D], F32R)
        w_vg = sb("w_vg", [D, 2, VD])
        w_vg_r = sb("w_vg_r", [D, 2, 2, VD], F32R)
        w_ret_o = sb("w_ret_o", [P, 2, D])
        w_ret = sb("w_ret", [P, 2, D])
        norm_w = sb("norm_w", [P, 1])
        w_x = sb("w_x", [D, 3, D])
        gate_w = sb("gate_w", [D, E])
        expert_w = sb("expert_w", [D, E * D])
        expert_r = sb("expert_r", [D, 2, E * D], F32R)
        comb_w = sb("comb_w", [D, D])
        tables = sb("tables", [D, 2, 2 * T])
        squares_in = sb("squares_in", [P, 2, P])
        cos_t, sin_t = tables[:, 0, :], tables[:, 1, :]
        ident, causal = squares_in[:, 0, :], squares_in[:, 1, :]
        ident16 = sb("ident16", [P, P], BF16)
        row_pick_in = sb("row_pick_in", [D, 2, XG, 3 * GR])
        row_pick = sb("row_pick", [D, 2, XG, 3 * GR], F32R)
        head_pick = sb("head_pick", [P, PAIRS, 2, XK])
        head_mask = sb("head_mask", [3 * GR, GH])
        iota_e = sb("iota_e", [P, E])
        ones_r = sb("ones_r", [64, P], F32R)
        bias_in = sb("bias_in", [64, E * D])
        bias_r = sb("bias_r", [64, E * D], F32R)
        minus_half = sb("minus_half", [P, J * RH])
        minus_one = sb("minus_one", [P, J])
        eps_ln = sb("eps_ln", [P, J])
        eps_sum = sb("eps_sum", [P, J * RH])
        ctxT = sb("ctxT", [D, (B + 1) * XK])
        w_k3 = sb("w_k3", [D, XG, 3 * GR])
        k_parts = sb("k_parts", [3 * GR, XG, B * XK], F32R)
        v_bd = sb("v_bd", [P, B, PAIRS, VW])
        v_now = sb("v_now", [P, PAIRS, 2 * VW])
        ones_now = sb("ones_now", [P, 3 * VW])
        xT = sb("xT", [D, T])
        xT_r = sb("xT_r", [D, 2, T], F32R)
        x_in = sb("x_in", [P, J, D])
        r_cos = sb("r_cos", [D, 2 * T])
        r_sin = sb("r_sin", [D, 2 * T])
        r_swap = sb("r_swap", [D, 2 * T])
        qk = sb("qk", [D, 2, T])
        k_head = sb("k_head", [D, RH, T])
        v = sb("v", [P, J, VD])
        g_tanh = sb("g_tanh", [P, J * VD])
        gate = sb("gate", [P, J * VD])
        p_diag = sb("p_diag", [P, J, RH, P])
        p_cross = sb("p_cross", [P, RH, P])
        squares = sb("squares", [P, J * RH, RV])
        ssq = sb("ssq", [P, J * RH])
        ssq_eps = sb("ssq_eps", [P, J * RH])
        rms = sb("rms", [P, J * RH])
        u = sb("u", [P, J * RH, RV])
        og = sb("og", [P, J, 2, P])
        ogT = sb("ogT", [P, J, 2, P])
        x1 = sb("x1", [P, J, D])
        x1_all = sb("x1_all", [P, B, J, D])
        x1T = sb("x1T", [D, T])
        q_r = sb("q_r", [D, 2, T], F32R)
        ln = [dict(sum=sb(f"ln{n}_sum", [P, J, D]), stats=sb(f"ln{n}_stats", [P, J, 6]),
                   mv=sb(f"ln{n}_mv", [P, J, 2]), var=sb(f"ln{n}_var", [P, J]),
                   tick=sb(f"ln{n}_tick", [P, 1]), rate=sb(f"ln{n}_rate", [P, J])) for n in range(3)]
        tick = sb("tick", [P, 1])
        neg_max = sb("neg_max", [P, J, XH])
        max16 = sb("max16", [P, J, 2 * XH], BF16)
        q_now = sb("q_now", [P, XG, T], F32R)
        k_now = sb("k_now", [P, PAIRS, 2, XK], F32R)
        k_tick = sb("k_tick", [P, 1])
        inv = sb("inv", [D, T])
        probsT = sb("probsT", [P, PAIRS, T])
        attT = sb("attT_sb", [D, T])
        x2 = sb("x2", [P, J, D])
        x2_all = sb("x2_all", [P, B, J, D])
        x2T = sb("x2T_sb", [D, T])
        x2T_all = sb("x2T_all", [D, B, T])
        lg = sb("lg", [P, J, E])
        top = sb("top", [P, J, 8])
        top_i = sb("top_i", [P, J, 8], U32)
        top_if = sb("top_if", [P, J, 2])
        top_d = sb("top_d", [P, J, 8])
        top_e = sb("top_e", [P, J, 8])
        top_s = sb("top_s", [P, J])
        top_r = sb("top_r", [P, J])
        top_p = sb("top_p", [P, J, 2])
        hot = sb("hot", [P, J, 2, E])
        w_hot = sb("w_hot", [P, J, 2, E])
        w_all = sb("w_all", [P, B, J, E])
        w_now = sb("w_now", [P, 2, J, E])
        x2T_now = sb("x2T_now", [D, T])
        y_r = sb("y_r", [D, 2, 2, T], F32R)
        h = sb("h", [P, 2, J, E, D])
        acc = sb("acc", [P, J, E, D])
        mixT_sb = sb("mixT_sb", [D, T])
        neg_mean = sb("neg_mean", [P, J])
        neg_shift = sb("neg_shift", [P, J])
        y = sb("y", [P, J, D])

        bank = ctx.enter_context(nc.psum_tensor("bank", [P, 8, 512], F32))
        H0, H1, R0, C0, XS, XA, XB = 0, 1, 2, 3, 4, 6, 7

        def one(t, n):
            return t[:, bass.ds(n, 1)].rearrange("p o a c -> p (o a) c")

        def halves(m):
            return bank[:, m, 0:T].rearrange("p (j d) -> p j d", j=J)

        def steady(engine, body):
            for i in range(STAGES):
                body(i)
            with engine.Fori(STAGES, B - 1) as i:
                body(i)
            for i in range(B - 1, B + STAGES - 1):
                body(i)

        def runs(i, lag):
            return not isinstance(i, int) or 0 <= i - lag < B

        def expert_steady(engine, body):
            for i in range(4):
                body(i, i % 2)
            with engine.Fori(2, B // 2) as pair:
                body(2 * pair, 0)
                body(2 * pair + 1, 1)
            for i in range(B, B + 3):
                body(i, i % 2)

        block = ctx.enter_context(nc.Block())

        @block.sync
        def _(sp):
            sp.dma_start(xT[:, :], a["xT"][:, 0:T]).then_inc(s["xT_loaded"], 16)
            sp.dma_start(w_vg[:, :, :], a["w_vg"]).then_inc(s["vg_w_loaded"], 16)
            sp.dma_start(tables[:, :, :], a["tables"]).then_inc(s["tables_loaded"], 16)
            sp.dma_start(squares_in[:, :, :], a["squares"]).then_inc(s["ident_loaded"], 16)
            sp.dma_start(w_x[:, :, :], a["w_x"]).then_inc(s["x_w_loaded"], 16)
            sp.dma_start(head_mask[:, :], a["head_mask"]).then_inc(s["pick_loaded"], 16)
            sp.dma_start(row_pick_in[:, :, :, :], a["row_pick"]).then_inc(s["pick_loaded"], 16)
            sp.dma_start(w_ret_o[:, :, :], a["w_ret_o"]).then_inc(s["out_w_loaded"], 16)
            sp.dma_start(norm_w[:, :], a["norm_w"]).then_inc(s["out_w_loaded"], 16)
            sp.dma_start(x_in[:, :, :], a["x"][0]).then_inc(s["x_loaded"], 16)
            sp.dma_start(head_pick[3 * GR:P, :, :, :], a["head_pick"]).then_inc(s["pick_loaded"], 16)
            sp.dma_start(iota_e[:, :], a["iota_e"]).then_inc(s["ffn_loaded"], 16)
            sp.dma_start(gate_w[:, :], a["gate_w"]).then_inc(s["ffn_loaded"], 16)
            sp.dma_start(bias_in[:, :], a["bias"]).then_inc(s["ffn_loaded"], 16)
            sp.dma_start(expert_w[:, :], a["expert_w"]).then_inc(s["ffn_loaded"], 16)
            sp.dma_start(comb_w[:, :], a["comb_w"]).then_inc(s["ffn_loaded"], 16)
            with sp.Fori(1, B) as b:
                sp.wait_ge(s["x_lo"], b)
                sp.dma_start(xT[:, :], a["xT"][:, bass.ds(b * T, T)]).then_inc(s["xT_loaded"], 16)
                sp.wait_ge(s["res1"], b)
                sp.dma_start(x_in[:, :, :], a["x"][bass.ds(b, 1)].rearrange("o p j d -> p (o j) d"))\
                  .then_inc(s["x_loaded"], 16)
            with sp.Fori(0, B) as b:
                sp.wait_ge(s["y_kept"], b + 1)
                sp.dma_start(out[bass.ds(b, 1)].rearrange("o p j d -> p (o j) d"), y[:, :, :]).then_inc(s["out_stored"], 16)
            sp.wait_ge(s["out_stored"], 16 * B)

        @block.gpsimd
        def _(pool):
            pool.memset(k_head[:, :, :], 0.0).then_inc(s["zeros_made"], 1)
            pool.memset(v_bd[:, :, :, :], 0.0).then_inc(s["zeros_made"], 1)
            pool.memset(v_now[:, :, :], 0.0).then_inc(s["zeros_made"], 1)
            pool.memset(ones_now[:, :], 0.0).then_inc(s["zeros_made"], 1)
            pool.memset(minus_half[:, :], -0.5).then_inc(s["consts_made"], 1)
            pool.memset(minus_one[:, :], -1.0).then_inc(s["consts_made"], 1)
            pool.memset(eps_ln[:, :], EPS).then_inc(s["consts_made"], 1)
            pool.memset(eps_sum[:, :], EPS * RV).then_inc(s["consts_made"], 1)
            pool.memset(ones_r[:, :].bitcast(F32), 1.0).then_inc(s["consts_made"], 1)

            def power(var, var_eps, rate, eps, ready, eps_done, done, n):
                pool.wait_ge(ready, n + 1)
                pool.tensor_tensor(var_eps, var, eps, ALU.add).then_inc(eps_done, 1)
                pool.wait_ge(eps_done, n + 1)
                pool.tensor_tensor(rate, var_eps, minus_half[:, 0:var.shape[-1]], ALU.pow).then_inc(done, 1)

            pool.wait_ge(s["pick_loaded"], 48)
            pool.tensor_copy(row_pick[:, :, :, :], row_pick_in[:, :, :, :]).then_inc(s["picks_made"], 1)

            def mask_keys(n):
                if isinstance(n, int) and n == 0:
                    pool.wait_ge(s["k_lo"], XG)
                else:
                    pool.wait_ge(s["scoresT1"], n)
                pool.tensor_tensor(k_tick[:, :], minus_one[:, 0:1], minus_one[:, 0:1], ALU.mult)
                pool.tensor_tensor(k_now[0:3 * GR, :, :, :].rearrange("p (g n) w k -> p g (n w) k", g=XG),
                                   k_parts[:, :, bass.ds(n * XK, XK)].bitcast(F32).unsqueeze(2).broadcast_to([3 * GR, XG, GH, XK]),
                                   head_mask[:, :].unsqueeze(1).unsqueeze(3).broadcast_to([3 * GR, XG, GH, XK]), ALU.mult)\
                    .then_inc(s["k_masked"], 1)

            def rms_rate(n):
                power(ssq[:, :], ssq_eps[:, :], rms[:, :], eps_sum[:, :], s["square_sums"], s["rms_eps"], s["rms_rate"], n)

            def norm_rate(n, k):
                power(ln[k - 1]["mv"][:, :, 1], ln[k - 1]["var"][:, :], ln[k - 1]["rate"][:, :], eps_ln[:, :],
                      s[f"moments{k}"], s[f"var{k}_eps"], s[f"rate{k}"], n)

            def hold_x1(n):
                pool.wait_ge(s["x1_kept"], n + 1)
                pool.tensor_copy(one(x1_all, n), x1[:, :, :]).then_inc(s["x1_held"], 1)

            def hold_x2(n):
                pool.wait_ge(s["x2_kept"], n + 1)
                pool.tensor_copy(one(x2_all, n), x2[:, :, :]).then_inc(s["x2_held"], 1)

            def hold_x2T(n):
                pool.wait_ge(s["x2T_kept"], n + 1)
                pool.tensor_copy(x2T_all[:, bass.ds(n, 1), :].rearrange("p o t -> p (o t)"), x2T[:, :]).then_inc(s["x2T_held"], 1)

            def place_v(n):
                if isinstance(n, int) and n == 0:
                    pool.wait_ge(s["vx_kept"], 5)
                else:
                    pool.wait_ge(s["av"], n)
                pool.tensor_copy(v_now[:, :, 0:VW], v_bd[:, bass.ds(n, 1), :, :].rearrange("p o m c -> p (o m) c")).then_inc(s["v_placed"], 1)

            def step(i):
                if runs(i, 1):
                    place_v(i - 1)
                if runs(i, 3):
                    hold_x2(i - 3)
                if runs(i, 0):
                    rms_rate(i)
                if runs(i, 1):
                    hold_x1(i - 1)
                if runs(i, 3):
                    hold_x2T(i - 3)
                if runs(i, 2):
                    norm_rate(i - 2, 2)
                if runs(i, 0):
                    norm_rate(i, 1)
                    mask_keys(i)

            pool.wait_ge(s["consts_made"], 5)
            steady(pool, step)

            def load(n, parity):
                wait(pool, s["y_hi"], n)
                wait(pool, s["y_lo"], n)
                pool.tensor_copy(x2T_now[:, :], x2T_all[:, bass.ds(n, 1), :].rearrange("p o t -> p (o t)")).then_inc(s["y_here"], 1)
                wait(pool, s["mixed1"], n - 1)
                pool.tensor_copy(w_now[:, parity, :, :], one(w_all, n)).then_inc(s["w_here"], 1)
                pool.wait_ge(s["y_hi"], n + 1)
                pool.tensor_tensor(y_r[:, parity, 1, :], x2T_now[:, :], y_r[:, parity, 0, :].bitcast(F32), ALU.subtract).then_inc(s["y_lo"], 1)

            def expert_step(i, parity):
                if runs(i, 0):
                    load(i, parity)
                if runs(i, 3):
                    power(ln[2]["mv"][:, :, 1], ln[2]["var"][:, :], ln[2]["rate"][:, :], eps_ln[:, :],
                          s["moments3"], s["var3_eps"], s["rate3"], i - 3)
                    pool.tensor_tensor(neg_mean[:, :], ln[2]["mv"][:, :, 0], minus_one[:, :], ALU.mult).then_inc(s["mean3"], 1)
                    pool.wait_ge(s["rate3"], i - 2)
                    pool.wait_ge(s["mean3"], i - 2)
                    pool.tensor_tensor(neg_shift[:, :], neg_mean[:, :], ln[2]["rate"][:, :], ALU.mult).then_inc(s["shift3"], 1)

            pool.wait_ge(s["x2T_held"], B)
            pool.wait_ge(s["w_kept"], B)
            expert_steady(pool, expert_step)

        @block.scalar
        def _(act):
            act.dma_start(w_qk[:, :, :], a["w_qk"]).then_inc(s["rope_w_loaded"], 16)
            act.dma_start(ctxT[:, :], a["ctxT"]).then_inc(s["ctx_loaded"], 16)
            act.dma_start(w_k3[:, :, :], a["w_k3"]).then_inc(s["ctx_loaded"], 16)
            act.preload_act_table_set("exp_and_others")

            def split_x(n):
                act.wait_ge(s["xT_loaded"], 16 * n + 16)
                wait(act, s["g_proj"], n)
                act.activation(xT_r[:, 0, :], xT[:, :], ACT.Copy).then_inc(s["x_hi"], 1)

            act.wait_ge(s["rope_w_loaded"], 16)
            act.activation(w_qk_r[:, 0, :, :], w_qk[:, :, :], ACT.Copy).then_inc(s["rope_w_hi"], 1)
            act.wait_ge(s["vg_w_loaded"], 16)
            act.activation(w_vg_r[:, 0, :, :], w_vg[:, :, :], ACT.Copy).then_inc(s["vg_w_hi"], 1)

            def keep_v(n):
                act.wait_ge(s["v_proj"], n + 1)
                wait(act, s["ret_out"], n)
                act.activation(v[:, :, :], bank[:, H1, :].rearrange("p (j n) -> p j n", j=J), ACT.Copy).then_inc(s["v_kept"], 1)

            def max_out(n):
                act.wait_ge(s["maxT"], n + 1)
                wait(act, s["scoresT1"], n)
                act.activation(q_now[3 * GR:P, :, :], bank[3 * GR:P, XS, 0:T // 2].bitcast(BF16).unsqueeze(1).broadcast_to([2 * XH, XG, T]),
                               ACT.Copy).then_inc(s["maxT_kept"], 1)

            def square(n):
                act.wait_ge(s["ret_out"], n + 1)
                wait(act, s["square_sums"], n)
                act.activation(squares[:, :, :], bank[:, R0, :].rearrange("p (n c) -> p n c", c=RV), ACT.Square).then_inc(s["squares"], 1)

            def exponent(n, half):
                act.wait_ge(s[f"scoresT{half}"], n + 1)
                wait(act, s["av"], n)
                m = (XA, XS)[half]
                act.activation(probsT[:, 4 * half:4 * half + 4, :], bank[:, m:m + 2, :].rearrange("p n (m t) -> p (n m) t", t=T),
                               ACT.Exp).then_inc(s[f"exp{half}"], 1)

            def spread_k(n):
                act.wait_ge(s["rotated"], n + 1)
                wait(act, s["score1"], n)
                if isinstance(n, int) and n == 0:
                    act.wait_ge(s["zeros_made"], 1)
                for m in range(RH):
                    r = slice(RK * m, RK * m + RK)
                    last = act.activation(k_head[r, m, :], qk[r, 1, :], ACT.Copy)
                last.then_inc(s["k_spread"], 1)

            def tanh(n):
                act.wait_ge(s["g_proj"], n + 1)
                wait(act, s["gate_kept"], n)
                act.activation(g_tanh[:, :], bank[:, H0, :], ACT.Tanh, scale=0.5).then_inc(s["gate_tanh"], 1)

            def g_out(n):
                act.wait_ge(s["gT"], n + 1)
                wait(act, s["ret_proj"], n)
                act.activation(ogT[:, :, :, :], bank[:, R0, :].rearrange("p (j n c) -> p j n c", j=J, n=2), ACT.Copy).then_inc(s["gT_kept"], 1)

            def cross_out(n):
                act.wait_ge(s["scorex"], n + 1)
                wait(act, s["ret_out"], n)
                act.activation(p_cross[:, :, :], bank[:, H0, :].rearrange("p (n c) -> p n c", c=P), ACT.Copy).then_inc(s["cross"], 1)

            def x2_out(n):
                act.wait_ge(s["x2T"], n + 1)
                wait(act, s["logits"], n)
                wait(act, s["x2T_held"], n)
                act.activation(x2T[:, :], bank[:, C0, 0:T], ACT.Copy).then_inc(s["x2T_kept"], 1)

            def logits_out(n):
                act.wait_ge(s["logits"], n + 1)
                wait(act, s["top_found"], n)
                act.activation(lg[:, :, :], bank[:, C0, 0:J * E].rearrange("p (j e) -> p j e", j=J), ACT.Copy).then_inc(s["logits_kept"], 1)

            def top_exp(n):
                act.wait_ge(s["top_found"], n + 1)
                wait(act, s["top_prob"], n)
                act.activation(top_e[:, :, :], top_d[:, :, :], ACT.Exp).then_inc(s["top_exp"], 1)

            def x1_out(n):
                act.wait_ge(s["x1T"], n + 1)
                wait(act, s["q_proj"], n)
                act.activation(x1T[:, :], bank[:, R0, 0:T], ACT.Copy).then_inc(s["x1T_kept"], 1)

            def query_hi(n):
                act.wait_ge(s["q_proj"], n + 1)
                wait(act, s["q_picked"], n)
                act.activation(q_r[:, 0, :], bank[:, R0, 0:T], ACT.Copy, scale=XD ** -0.5).then_inc(s["q_hi"], 1)

            def spread_q(n):
                act.wait_ge(s["q_picked"], n + 1)
                wait(act, s["scoresT1"], n)
                act.activation(q_now[0:3 * GR, :, :], bank[0:3 * GR, XA:XA + 2, :].rearrange("p n (m t) -> p (n m) t", t=T),
                               ACT.Copy).then_inc(s["q_spread"], 1)

            def context():
                for g in range(XG):
                    act.wait_ge(s["k_proj"], g + 1)
                    act.activation(k_parts[:, g, :], bank[0:3 * GR, R0 + g, :], ACT.Copy).then_inc(s["k_hi"], 1)
                act.wait_ge(s["zeros_made"], 4)
                act.wait_ge(s["vx_proj"], B)
                for m in range(2):
                    for half in range(2):
                        lo = XK * half
                        src = bank[lo:lo + XK, XA + m, :].rearrange("p (b n w c) -> p b n w c", n=PAIRS, w=2, c=XD)[:, :, :, half, :]
                        first = 4 * m + half
                        count = min(4, B - first)
                        act.activation(v_bd[lo:lo + XK, first:first + count, :, XD * half:XD * half + XD], src[:, 0:count], ACT.Copy)\
                           .then_inc(s["vx_kept"], 1)
                act.activation(v_bd[XK:P, 0:1, :, XD:2 * XD], src[:, 3:4], ACT.Copy).then_inc(s["vx_kept"], 1)

            def step(i):
                if runs(i, 2):
                    g_out(i - 2)
                if runs(i, 3):
                    exponent(i - 3, 0)
                    exponent(i - 3, 1)
                if runs(i, 0):
                    split_x(i)
                if runs(i, 1):
                    cross_out(i - 1)
                if runs(i, 2):
                    x1_out(i - 2)
                if runs(i, 4):
                    x2_out(i - 4)
                if runs(i, 2):
                    query_hi(i - 2)
                if runs(i, 4):
                    logits_out(i - 4)
                if runs(i, 2):
                    spread_q(i - 2)
                if runs(i, 1):
                    square(i - 1)
                if runs(i, 0):
                    keep_v(i)
                if runs(i, 4):
                    top_exp(i - 4)
                if runs(i, 0):
                    tanh(i)
                    spread_k(i)
                if runs(i, 2):
                    max_out(i - 2)
                if isinstance(i, int) and i == 0:
                    context()

            steady(act, step)

            def silu(n, parity, j):
                act.wait_ge(s[f"z{j}"], n + 1)
                wait(act, s[f"mixed{j}"], n - 1)
                act.activation(h[:, parity, j, :, :], bank[:, 2 * j:2 * j + 2, :].rearrange("p n (e d) -> p (n e) d", d=D), ACT.Silu)\
                   .then_inc(s[f"h{j}"], 1)

            def high_y(n, parity):
                act.wait_ge(s["y_here"], n + 1)
                wait(act, s["z1"], n - 1)
                act.activation(y_r[:, parity, 0, :], x2T_now[:, :], ACT.Copy).then_inc(s["y_hi"], 1)

            def mixed_out(n):
                act.wait_ge(s["mixT"], n + 1)
                wait(act, s["comb"], n)
                act.activation(mixT_sb[:, :], bank[:, 4, 0:T], ACT.Copy).then_inc(s["mixT_kept"], 1)

            def last_norm(n):
                act.wait_ge(s["rate3"], n + 1)
                act.wait_ge(s["shift3"], n + 1)
                wait(act, s["out_stored"], 16 * n)
                for j in range(J):
                    last = act.activation(y[:, j, :], ln[2]["sum"][:, j, :], ACT.Identity, bias=neg_shift[:, j:j + 1],
                                          scale=ln[2]["rate"][:, j:j + 1])
                last.then_inc(s["y_kept"], 1)

            def expert_step(i, parity):
                if runs(i, 3):
                    mixed_out(i - 3)
                if runs(i, 1):
                    silu(i - 1, 1 - parity, 0)
                if runs(i, 0):
                    high_y(i, parity)
                if runs(i, 1):
                    silu(i - 1, 1 - parity, 1)
                if runs(i, 3):
                    last_norm(i - 3)

            expert_steady(act, expert_step)

        @block.vector
        def _(dve):
            def layer_norm(n, k, add_a, add_b):
                t = ln[k - 1]
                wait(dve, s[("x1_kept", "x2_kept", "y_kept")[k - 1]], n)
                dve.tensor_tensor(t["sum"][:, :, :], add_a, add_b, ALU.add).then_inc(s[f"res{k}"], 1)
                dve.wait_ge(s[f"res{k}"], n + 1)
                for j in range(J):
                    last = dve.bn_stats(t["stats"][:, j, :], t["sum"][:, j, :])
                last.then_inc(s[f"stats{k}"], 1)
                dve.wait_ge(s[f"stats{k}"], n + 1)
                dve.memset(t["tick"][:, :], 0.0)
                for j in range(J):
                    last = dve.bn_aggr(t["mv"][:, j, :], t["stats"][:, j, :])
                last.then_inc(s[f"moments{k}"], 1)

            def normalise(n, k, dst, name):
                t = ln[k - 1]
                dve.wait_ge(s[f"rate{k}"], n + 1)
                for j in range(J):
                    last = dve.tensor_scalar(dst[:, j, :], t["sum"][:, j, :], t["mv"][:, j, 0:1], t["rate"][:, j:j + 1],
                                             ALU.subtract, ALU.mult)
                last.then_inc(s[f"{name}_kept"], 1)

            def low_x(n):
                dve.wait_ge(s["x_hi"], n + 1)
                dve.tensor_tensor(xT_r[:, 1, :], xT[:, :], xT_r[:, 0, :].bitcast(F32), ALU.subtract).then_inc(s["x_lo"], 1)

            def rope_multiply(n):
                dve.wait_ge(s["qk_proj"], n + 1)
                dve.tensor_tensor(r_sin[:, :], bank[:, H0, :], sin_t, ALU.mult).then_inc(s["rope_sin"], 1)
                dve.tensor_tensor(r_cos[:, :], bank[:, H0, :], cos_t, ALU.mult).then_inc(s["rope_cos"], 1)

            def rope_swap(n):
                dve.wait_ge(s["rope_sin"], n + 1)
                dve.memset(tick[:, :], 0.0)
                dve.stream_shuffle(r_swap[:, :], r_sin[:, :], [(p + RK // 2) % RK for p in range(32)]).then_inc(s["rope_swap"], 1)

            def rope_add(n):
                dve.wait_ge(s["rope_cos"], n + 1)
                dve.wait_ge(s["rope_swap"], n + 1)
                wait(dve, s["score1"], n)
                dve.tensor_tensor(qk[:, :, :].rearrange("p a t -> p (a t)"), r_cos[:, :], r_swap[:, :], ALU.add).then_inc(s["rotated"], 1)

            def gates(n):
                dve.wait_ge(s["gate_tanh"], n + 1)
                wait(dve, s["gated"], n)
                dve.scalar_tensor_tensor(gate[:, :], g_tanh[:, :], 1.0, bank[:, H0, :], ALU.add, ALU.mult).then_inc(s["gate_kept"], 1)

            def diagonal(n, k):
                dve.wait_ge(s[f"score{k}"], n + 1)
                wait(dve, s["ret_out"], n)
                dve.tensor_tensor(p_diag[:, k, :, :], bank[:, H1, :].rearrange("p (n c) -> p n c", c=P),
                                  causal.unsqueeze(1).broadcast_to([P, RH, P]), ALU.mult).then_inc(s[f"diag{k}"], 1)

            def gated(n):
                dve.wait_ge(s["squares"], n + 1)
                dve.tensor_tensor(u[:, :, :], gate[:, :].rearrange("p (n c) -> p n c", c=RV),
                                  bank[:, R0, :].rearrange("p (n c) -> p n c", c=RV), ALU.mult).then_inc(s["gated"], 1)

            def square_sums(n):
                dve.wait_ge(s["squares"], n + 1)
                wait(dve, s["rms_eps"], n)
                dve.tensor_reduce(ssq[:, :], squares[:, :, :], AX.X, ALU.add).then_inc(s["square_sums"], 1)

            def scale_rms(n):
                dve.wait_ge(s["rms_rate"], n + 1)
                dve.wait_ge(s["gated"], n + 1)
                wait(dve, s["gT"], n)
                dve.tensor_tensor(og[:, :, :, :].rearrange("p j n (m c) -> p (j n m) c", c=RV), u[:, :, :],
                                  rms[:, :].unsqueeze(2).broadcast_to([P, J * RH, RV]), ALU.mult).then_inc(s["scaled"], 1)

            def norm1(n):
                dve.wait_ge(s["ret_proj"], n + 1)
                dve.wait_ge(s["x_loaded"], 16 * n + 16)
                layer_norm(n, 1, halves(R0), x_in[:, :, :])

            def norm1_end(n):
                wait(dve, s["x1T"], n)
                wait(dve, s["x1_held"], n)
                normalise(n, 1, x1, "x1")

            def query_lo(n):
                dve.wait_ge(s["q_hi"], n + 1)
                dve.scalar_tensor_tensor(q_r[:, 1, :], bank[:, R0, 0:T], XD ** -0.5, q_r[:, 0, :].bitcast(F32),
                                         ALU.mult, ALU.subtract).then_inc(s["q_lo"], 1)

            def maximum(n, j):
                dve.wait_ge(s[f"max_scores{j}"], n + 1)
                wait(dve, s["max_lo"], n)
                m = (XS, XA)[j]
                dve.tensor_reduce(neg_max[:, j, :], bank[:, m:m + 2, :].rearrange("p n (h k) -> p (n h) k", k=XK),
                                  AX.X, ALU.max, negate=True).then_inc(s[f"max{j}"], 1)

            def max_hi(n):
                dve.wait_ge(s["max0"], n + 1)
                dve.wait_ge(s["max1"], n + 1)
                wait(dve, s["maxT"], n)
                dve.tensor_copy(max16[:, :, 0:XH], neg_max[:, :, :]).then_inc(s["max_hi"], 1)

            def max_lo(n):
                dve.wait_ge(s["max_hi"], n + 1)
                dve.tensor_tensor(max16[:, :, XH:2 * XH], neg_max[:, :, :], max16[:, :, 0:XH], ALU.subtract).then_inc(s["max_lo"], 1)

            def invert(n):
                dve.wait_ge(s["av"], n + 1)
                wait(dve, s["att"], n)
                dve.reciprocal(inv[:, :], bank[:, XA, T:2 * T]).then_inc(s["inv"], 1)

            def attended(n):
                dve.wait_ge(s["inv"], n + 1)
                wait(dve, s["x_proj"], n)
                dve.tensor_tensor(attT[:, :], bank[:, XA, 0:T], inv[:, :], ALU.mult).then_inc(s["att"], 1)

            def norm2(n):
                dve.wait_ge(s["x_proj"], n + 1)
                dve.wait_ge(s["x1_held"], n + 1)
                layer_norm(n, 2, halves(C0), one(x1_all, n))

            def norm2_end(n):
                wait(dve, s["x2T"], n)
                wait(dve, s["x2_held"], n)
                normalise(n, 2, x2, "x2")

            def gating_1(n):
                dve.wait_ge(s["logits_kept"], n + 1)
                wait(dve, s["top_inv"], n)
                dve.memset(tick[:, :], 0.0)
                for j in range(J):
                    last = dve.max(top[:, j, :], lg[:, j, :])
                last.then_inc(s["top_max"], 1)

            def gating_2(n):
                dve.wait_ge(s["top_max"], n + 1)
                wait(dve, s["top_exp"], n)
                dve.tensor_tensor(top_d[:, :, :], top[:, :, :], top[:, :, 0:1].broadcast_to([P, J, 8]), ALU.subtract)
                for j in range(J):
                    last = dve.max_index(top_i[:, j, :], top[:, j, :], lg[:, j, :])
                last.then_inc(s["top_found"], 1)

            def gating_3(n):
                dve.wait_ge(s["top_found"], n + 1)
                dve.tensor_copy(top_if[:, :, :], top_i[:, :, 0:2])
                dve.wait_ge(s["top_exp"], n + 1)
                dve.tensor_reduce(top_s[:, :], top_e[:, :, :], AX.X, ALU.add).then_inc(s["top_sum"], 1)

            def gating_4(n):
                dve.wait_ge(s["top_sum"], n + 1)
                dve.tensor_tensor(hot[:, :, :, :], iota_e[:, :].unsqueeze(1).unsqueeze(1).broadcast_to([P, J, 2, E]),
                                  top_if[:, :, :].unsqueeze(3).broadcast_to([P, J, 2, E]), ALU.is_equal)
                dve.reciprocal(top_r[:, :], top_s[:, :]).then_inc(s["top_inv"], 1)

            def gating_5(n):
                dve.wait_ge(s["top_inv"], n + 1)
                dve.tensor_tensor(top_p[:, :, :], top_e[:, :, 0:2], top_r[:, :].unsqueeze(2).broadcast_to([P, J, 2]), ALU.mult).then_inc(s["top_prob"], 1)

            def gating_6(n):
                dve.wait_ge(s["top_prob"], n + 1)
                dve.tensor_tensor(w_hot[:, :, :, :], hot[:, :, :, :], top_p[:, :, :].unsqueeze(3).broadcast_to([P, J, 2, E]), ALU.mult).then_inc(s["weighted"], 1)

            def gating_7(n):
                dve.wait_ge(s["weighted"], n + 1)
                dve.tensor_tensor(one(w_all, n), w_hot[:, :, 0, :], w_hot[:, :, 1, :], ALU.add).then_inc(s["w_kept"], 1)

            def step(i):
                if runs(i, 1):
                    diagonal(i - 1, 1)
                if runs(i, 0):
                    rope_multiply(i)
                if runs(i, 4):
                    gating_2(i - 4)
                if runs(i, 0):
                    rope_swap(i)
                    rope_add(i)
                if runs(i, 2):
                    maximum(i - 2, 0)
                if runs(i, 1):
                    square_sums(i - 1)
                if runs(i, 2):
                    maximum(i - 2, 1)
                    max_hi(i - 2)
                if runs(i, 1):
                    gated(i - 1)
                if runs(i, 2):
                    max_lo(i - 2)
                if runs(i, 1):
                    scale_rms(i - 1)
                if runs(i, 3):
                    norm2(i - 3)
                if runs(i, 4):
                    gating_3(i - 4)
                    gating_4(i - 4)
                if runs(i, 0):
                    gates(i)
                if runs(i, 3):
                    norm2_end(i - 3)
                if runs(i, 1):
                    norm1(i - 1)
                if runs(i, 4):
                    gating_5(i - 4)
                if runs(i, 0):
                    diagonal(i, 0)
                if runs(i, 1):
                    norm1_end(i - 1)
                if runs(i, 2):
                    invert(i - 2)
                if runs(i, 4):
                    gating_6(i - 4)
                if runs(i, -1):
                    low_x(i + 1)
                if runs(i, 2):
                    attended(i - 2)
                if runs(i, 1):
                    query_lo(i - 1)
                if runs(i, 4):
                    gating_7(i - 4)
                if runs(i, 3):
                    gating_1(i - 3)
                if isinstance(i, int) and i == 0:
                    for half in range(2):
                        dve.memset(ones_now[XK * half:XK * half + XK, VW + XD * half:VW + XD * half + XD], 1.0).then_inc(s["v_ones"], 1)
                    for g in range(XG):
                        dve.wait_ge(s["k_hi"], g + 1)
                        low = slice(2 * GR, 3 * GR)
                        dve.tensor_tensor(k_parts[low, g, :], bank[low, R0 + g, 0:B * XK], k_parts[low, g, :].bitcast(F32), ALU.subtract).then_inc(s["k_lo"], 1)
                    dve.wait_ge(s["pick_loaded"], 48)
                    dve.tensor_copy(k_now[3 * GR:P, :, :, :], head_pick[3 * GR:P, :, :, :]).then_inc(s["picks_made"], 1)
                if isinstance(i, int) and i == 1:
                    dve.wait_ge(s["ffn_loaded"], 80)
                    dve.tensor_copy(bias_r[:, :], bias_in[:, :])
                    dve.tensor_copy(expert_r[:, 0, :], expert_w[:, :]).then_inc(s["expert_hi"], 1)
                    dve.wait_ge(s["expert_hi"], 1)
                    dve.tensor_tensor(expert_r[:, 1, :], expert_w[:, :], expert_r[:, 0, :].bitcast(F32), ALU.subtract)
                    dve.tensor_tensor(bias_r[32:64, :], bias_in[32:64, :], bias_r[32:64, :].bitcast(F32), ALU.subtract).then_inc(s["bias_lo"], 1)

            low_x(0)
            dve.wait_ge(s["rope_w_hi"], 1)
            dve.tensor_tensor(w_qk_r[:, 1, :, :], w_qk[:, :, :], w_qk_r[:, 0, :, :].bitcast(F32), ALU.subtract).then_inc(s["weights_made"], 1)
            dve.wait_ge(s["vg_w_hi"], 1)
            dve.tensor_tensor(w_vg_r[:, 1, :, :], w_vg[:, :, :], w_vg_r[:, 0, :, :].bitcast(F32), ALU.subtract).then_inc(s["weights_made"], 1)
            dve.wait_ge(s["ident_loaded"], 16)
            dve.tensor_copy(ident16[:, :], ident).then_inc(s["weights_made"], 1)
            dve.wait_ge(s["out_w_loaded"], 32)
            dve.tensor_scalar(w_ret[:, :, :], w_ret_o[:, :, :], norm_w[:, 0:1], 0.5 * RV ** 0.5, ALU.mult, ALU.mult).then_inc(s["weights_made"], 1)
            dve.wait_ge(s["tables_loaded"], 16)
            steady(dve, step)

            def mix(n, parity):
                dve.wait_ge(s["w_here"], n + 1)
                dve.wait_ge(s["h0"], n + 1)
                dve.wait_ge(s["h1"], n + 1)
                wait(dve, s["mixT"], n)
                for e in range(E):
                    for j in range(J):
                        w = w_now[:, parity, j, e:e + 1]
                        if e == 0:
                            dve.tensor_scalar(acc[:, j, 0, :], h[:, parity, j, 0, :], w, None, ALU.mult).then_inc(mix_done[j][0], 1)
                        else:
                            dve.wait_ge(mix_done[j][e - 1], n + 1)
                            dve.scalar_tensor_tensor(acc[:, j, e, :], h[:, parity, j, e, :], w, acc[:, j, e - 1, :], ALU.mult, ALU.add)\
                               .then_inc(mix_done[j][e] if e < E - 1 else s[f"mixed{j}"], 1)

            def expert_step(i, parity):
                if runs(i, 2):
                    mix(i - 2, parity)
                if runs(i, 3):
                    dve.wait_ge(s["comb"], i - 2)
                    layer_norm(i - 3, 3, halves(5), one(x2_all, i - 3))

            expert_steady(dve, expert_step)

        @block.tensor
        def _(pe):
            def mm(o, l, r, start=True, stop=True, **k):
                return pe.matmul(o, l, r, start=start, stop=stop, **k)

            def mm3(o, left, right):
                mm(o, left(0), right(0), stop=False)
                mm(o, left(0), right(1), start=False, stop=False)
                return mm(o, left(1), right(0), start=False)

            def project_qk(n):
                pe.wait_ge(s["x_hi"], n + 1)
                pe.wait_ge(s["x_lo"], n + 1)
                wait(pe, s["cross"], n)
                for m in range(2):
                    last = mm3(bank[:, H0, m * T:(m + 1) * T], lambda k: w_qk_r[:, k, m, :], lambda k: xT_r[:, k, :])
                last.then_inc(s["qk_proj"], 1)

            def project_vg(n, m):
                if m == 0:
                    wait(pe, s["diag1"], n)
                else:
                    pe.wait_ge(s["rope_cos"], n + 1)
                for j in range(J):
                    last = mm3(bank[:, (H1, H0)[m], j * VD:(j + 1) * VD], lambda k: xT_r[:, k, j * P:(j + 1) * P],
                               lambda k: w_vg_r[:, k, m, :])
                last.then_inc(s[("v_proj", "g_proj")[m]], 1)

            def ret_scores(n, k):
                sc, tq, name = ((0, 0, "score0"), (1, 1, "score1"), (0, 1, "scorex"))[k]
                if k == 0:
                    pe.wait_ge(s["k_spread"], n + 1)
                    pe.wait_ge(s["v_kept"], n + 1)
                elif k == 2:
                    pe.wait_ge(s["gate_kept"], n + 1)
                else:
                    pe.wait_ge(s["diag0"], n + 1)
                for m in range(RH):
                    last = mm(bank[:, H0 if k == 2 else H1, m * P:(m + 1) * P], k_head[:, m, sc * P:(sc + 1) * P],
                              qk[:, 0, tq * P:(tq + 1) * P])
                last.then_inc(s[name], 1)

            def ret_out(n):
                pe.wait_ge(s["diag0"], n + 1)
                pe.wait_ge(s["diag1"], n + 1)
                pe.wait_ge(s["cross"], n + 1)
                pe.wait_ge(s["v_kept"], n + 1)
                wait(pe, s["q_lo"], n)
                for m in range(RH):
                    vm = slice(m * RV, (m + 1) * RV)
                    o = bank[:, R0, m * RV:(m + 1) * RV]
                    mm(o, p_diag[:, 0, m, :], v[:, 0, vm])
                    o = bank[:, R0, VD + m * RV:VD + (m + 1) * RV]
                    mm(o, p_cross[:, m, :], v[:, 0, vm], stop=False)
                    last = mm(o, p_diag[:, 1, m, :], v[:, 1, vm], start=False)
                last.then_inc(s["ret_out"], 1)

            def g_T(n):
                pe.wait_ge(s["scaled"], n + 1)
                for k in range(2 * J):
                    last = pe.transpose(bank[:, R0, k * P:(k + 1) * P], og[:, k // 2, k % 2, :], ident)
                last.then_inc(s["gT"], 1)

            def ret_proj(n):
                pe.wait_ge(s["gT_kept"], n + 1)
                for j in range(J):
                    for m in range(2):
                        last = mm(bank[:, R0, j * P:(j + 1) * P], ogT[:, j, m, :], w_ret[:, m, :], start=m == 0, stop=m == 1)
                last.then_inc(s["ret_proj"], 1)

            def x1_T(n):
                pe.wait_ge(s["x1_kept"], n + 1)
                for j in range(J):
                    last = pe.transpose(bank[:, R0, j * P:(j + 1) * P], x1[:, j, :], ident)
                last.then_inc(s["x1T"], 1)

            def query(n):
                pe.wait_ge(s["x1T_kept"], n + 1)
                mm(bank[:, R0, 0:T], w_x[:, 0, :], x1T[:, :]).then_inc(s["q_proj"], 1)

            def pick_q(n):
                pe.wait_ge(s["q_lo"], n + 1)
                wait(pe, s["att"], n)
                for g in range(XG):
                    o = bank[0:3 * GR, XA + g // 2, (g % 2) * T:(g % 2) * T + T]
                    mm(o, row_pick[:, 0, g, :], q_r[:, 0, :], stop=False)
                    last = mm(o, row_pick[:, 1, g, :], q_r[:, 1, :], start=False)
                last.then_inc(s["q_picked"], 1)

            def max_scores(n, j):
                if j == 0:
                    pe.wait_ge(s["q_spread"], n + 1)
                    pe.wait_ge(s["k_masked"], n + 1)
                    wait(pe, s["exp1"], n)
                for g in range(XG):
                    last = mm(bank[:, (XS, XA)[j] + g // 2, (g % 2) * T:(g % 2) * T + T], q_now[0:3 * GR, g, j * P:(j + 1) * P],
                              k_now[0:3 * GR, 2 * g:2 * g + 2, :, :].rearrange("p n w k -> p (n w k)"))
                last.then_inc(s[f"max_scores{j}"], 1)

            def max_T(n):
                pe.wait_ge(s["max_lo"], n + 1)
                for j in range(J):
                    last = pe.transpose(bank[3 * GR:P, XS, j * P // 2:(j + 1) * P // 2].bitcast(BF16), max16[:, j, :], ident16[:, :],
                                        tile_position=(0, 3 * GR))
                last.then_inc(s["maxT"], 1)

            def scores_T(n, half):
                pe.wait_ge(s["maxT_kept"], n + 1)
                for m in range(PAIRS // 2):
                    pair = PAIRS // 2 * half + m
                    last = mm(bank[:, (XA, XS)[half] + m // 2, (m % 2) * T:(m % 2) * T + T], k_now[:, pair, :, :].rearrange("p w k -> p (w k)"),
                              q_now[:, pair // 2, :])
                last.then_inc(s[f"scoresT{half}"], 1)

            def values(n):
                pe.wait_ge(s["exp0"], n + 1)
                pe.wait_ge(s["exp1"], n + 1)
                pe.wait_ge(s["v_placed"], n + 1)
                v_cols = v_now[:, :, :].rearrange("p m c -> p (m c)")
                for what in range(2):
                    for odd in range(2):
                        for k in range(PAIRS // 2):
                            m = 2 * k + odd
                            at = 2 * VW * m - VW * odd
                            left = ones_now[:, VW - VW * odd:3 * VW - VW * odd] if what else v_cols[:, at:at + 2 * VW]
                            last = mm(bank[32 * k:32 * k + 32, XA, T * what:T * what + T], left, probsT[:, m, :],
                                      start=odd == 0, stop=odd == 1, tile_position=(0, 32 * k))
                last.then_inc(s["av"], 1)

            def x_proj(n):
                pe.wait_ge(s["att"], n + 1)
                wait(pe, s["logits_kept"], n)
                for j in range(J):
                    last = mm(bank[:, C0, j * P:(j + 1) * P], attT[:, j * P:(j + 1) * P], w_x[:, 2, :])
                last.then_inc(s["x_proj"], 1)

            def x2_T(n):
                pe.wait_ge(s["x2_kept"], n + 1)
                for j in range(J):
                    last = pe.transpose(bank[:, C0, j * P:(j + 1) * P], x2[:, j, :], ident)
                last.then_inc(s["x2T"], 1)

            def logits(n):
                pe.wait_ge(s["x2T_kept"], n + 1)
                for j in range(J):
                    last = mm(bank[:, C0, j * E:(j + 1) * E], x2T[:, j * P:(j + 1) * P], gate_w[:, :])
                last.then_inc(s["logits"], 1)

            def context():
                pe.wait_ge(s["ctx_loaded"], 32)
                for g in range(XG):
                    mm(bank[0:3 * GR, R0 + g, :], w_k3[:, g, :], ctxT[:, 0:B * XK]).then_inc(s["k_proj"], 1)
                pe.wait_ge(s["x_w_loaded"], 16)
                for b in range(B):
                    mm(bank[:, XA + b // 4, b % 4 * D:b % 4 * D + D], ctxT[:, b * XK:(b + 2) * XK], w_x[:, 1, :]).then_inc(s["vx_proj"], 1)

            def step(i):
                if isinstance(i, int) and i == 1:
                    pe.wait_ge(s["k_lo"], XG)
                if isinstance(i, int) and i == 2:
                    pe.wait_ge(s["v_ones"], 2)
                    pe.wait_ge(s["vx_kept"], 5)
                    pe.wait_ge(s["picks_made"], 2)
                if runs(i, 3):
                    scores_T(i - 3, 0)
                    scores_T(i - 3, 1)
                if runs(i, 2):
                    ret_proj(i - 2)
                if runs(i, 1):
                    ret_scores(i - 1, 2)
                if runs(i, 3):
                    values(i - 3)
                if runs(i, 4):
                    x2_T(i - 4)
                if runs(i, 2):
                    x1_T(i - 2)
                if runs(i, 1):
                    ret_scores(i - 1, 1)
                if runs(i, 2):
                    query(i - 2)
                if runs(i, 4):
                    logits(i - 4)
                if runs(i, 0):
                    project_qk(i)
                if isinstance(i, int) and i == 0:
                    pe.wait_ge(s["weights_made"], 4)
                if runs(i, 2):
                    pick_q(i - 2)
                if runs(i, 1):
                    ret_out(i - 1)
                if runs(i, 2):
                    max_scores(i - 2, 0)
                if runs(i, 0):
                    project_vg(i, 0)
                    project_vg(i, 1)
                if isinstance(i, int) and i == 0:
                    context()
                if runs(i, 2):
                    max_scores(i - 2, 1)
                if runs(i, 3):
                    x_proj(i - 3)
                if runs(i, 0):
                    ret_scores(i, 0)
                if runs(i, 2):
                    max_T(i - 2)
                if runs(i, 1):
                    g_T(i - 1)

            pe.wait_ge(s["weights_made"], 1)
            steady(pe, step)

            def experts(n, parity, j):
                pe.wait_ge(s["y_hi"], n + 1)
                pe.wait_ge(s["y_lo"], n + 1)
                wait(pe, s[f"h{j}"], n)
                for m in range(2):
                    o = bank[:, 2 * j + m, :]
                    cols = slice(m * 512, (m + 1) * 512)
                    hi, lo = (y_r[:, parity, part, j * P:(j + 1) * P] for part in range(2))
                    mm(o, hi, expert_r[:, 0, cols], stop=False)
                    mm(o, hi, expert_r[:, 1, cols], start=False, stop=False)
                    mm(o, lo, expert_r[:, 0, cols], start=False, stop=False)
                    last = mm(o, ones_r[:, :], bias_r[:, cols], start=False)
                last.then_inc(s[f"z{j}"], 1)

            def mixed_T(n):
                pe.wait_ge(s["mixed0"], n + 1)
                pe.wait_ge(s["mixed1"], n + 1)
                wait(pe, s["mixT_kept"], n)
                for j in range(J):
                    last = pe.transpose(bank[:, 4, j * P:(j + 1) * P], acc[:, j, E - 1, :], ident)
                last.then_inc(s["mixT"], 1)

            def combine(n):
                pe.wait_ge(s["mixT_kept"], n + 1)
                wait(pe, s["res3"], n)
                for j in range(J):
                    last = mm(bank[:, 5, j * P:(j + 1) * P], mixT_sb[:, j * P:(j + 1) * P], comb_w[:, :])
                last.then_inc(s["comb"], 1)

            def expert_step(i, parity):
                if runs(i, 3):
                    mixed_T(i - 3)
                if runs(i, 1):
                    experts(i - 1, 1 - parity, 0)
                if runs(i, 3):
                    combine(i - 3)
                if runs(i, 1):
                    experts(i - 1, 1 - parity, 1)

            pe.wait_ge(s["bias_lo"], 1)
            pe.wait_ge(s["logits_kept"], B)
            expert_steady(pe, expert_step)


def constants():
    import numpy as np
    half = RK // 2
    inv_freq = (1.0 / np.float32(10000.0) ** (np.arange(0, RK, 2, dtype=np.float32) / np.float32(RK))).astype(np.float32)
    angle = (np.arange(T, dtype=np.float32)[None, :] * inv_freq[:, None]).astype(np.float64)
    cos, sin = np.cos(angle), np.sin(angle)
    log_decay = np.log1p(-np.exp2(-5.0 - np.arange(RH)))[:, None, None] * np.arange(T)[None, None, :]
    cos_h = np.broadcast_to(np.concatenate([cos, cos])[None], (RH, RK, T))
    sin_h = np.broadcast_to(np.concatenate([sin, -sin])[None], (RH, RK, T))
    up, down = np.exp(log_decay) * RK ** -0.5, np.exp(-log_decay)
    c = {}
    c["cos_t"] = np.stack([cos_h * up, cos_h * down], axis=2).reshape(D, 2 * T).astype(np.float32)
    c["sin_t"] = np.stack([sin_h * up, sin_h * down], axis=2).reshape(D, 2 * T).astype(np.float32)
    c["causal"] = (np.arange(P)[:, None] <= np.arange(P)[None, :]).astype(np.float32)
    c["ident"] = np.eye(P, dtype=np.float32)
    c["head_mask"] = (np.arange(3 * GR)[:, None] % GR // XD == np.arange(GH)[None, :]).astype(np.float32)
    c["head_pick"] = (np.arange(2 * XH)[:, None] % XH == np.arange(XH * XK)[None, :] // XK).astype(np.float32).reshape(2 * XH, PAIRS, 2, XK)
    pick = np.zeros((D, 2, XG, 3, GR), np.float32)
    for third, part in enumerate((0, 1, 0)):
        pick[:, part, :, third, :] = np.eye(D, dtype=np.float32).reshape(D, XG, GR)
    c["row_pick"] = pick.reshape(D, 2, XG, 3 * GR)
    c["iota_e"] = np.broadcast_to(np.arange(E, dtype=np.float32), (P, E)).copy()
    return c


def kernel(x, ctx_1024, L0_attn_Wq, L0_attn_Wk, L0_attn_Wv, L0_attn_Wg, L0_attn_Wo, L0_attn_g_norm_w,
           L0_xattn_w_q, L0_xattn_w_k, L0_xattn_w_v, L0_xattn_w_o,
           L0_ffn_gate_w, L0_ffn_expert_w, L0_ffn_expert_b, L0_ffn_combine_w):
    import numpy as np
    import concourse.bacc as bacc
    from concourse.bass_utils import run_bass_kernel_spmd

    x = np.asarray(x)
    wq, wk = np.asarray(L0_attn_Wq), np.asarray(L0_attn_Wk)
    bias = np.zeros((64, E * D), np.float32)
    bias[0] = bias[32] = np.asarray(L0_ffn_expert_b).reshape(-1)
    arrays = constants()
    arrays["tables"] = np.stack([arrays.pop("cos_t"), arrays.pop("sin_t")], axis=1)
    arrays["squares"] = np.stack([arrays.pop("ident"), arrays.pop("causal")], axis=1)
    arrays["xT"] = x.reshape(B * T, D).T
    arrays["x"] = x.reshape(B, J, P, D).transpose(0, 2, 1, 3)
    arrays["w_qk"] = np.stack([wq.T, wk.T], axis=1)
    arrays["w_vg"] = np.stack([np.asarray(L0_attn_Wv).T, np.asarray(L0_attn_Wg).T], axis=1)
    arrays["w_ret_o"] = np.asarray(L0_attn_Wo).T.reshape(2, P, D).transpose(1, 0, 2)
    arrays["norm_w"] = np.tile(np.asarray(L0_attn_g_norm_w), P // RV).reshape(P, 1)
    arrays["w_x"] = np.stack([np.asarray(w).T for w in (L0_xattn_w_q, L0_xattn_w_v, L0_xattn_w_o)], axis=1)
    arrays["w_k3"] = np.repeat(np.asarray(L0_xattn_w_k).T.reshape(D, XG, 1, GR), 3, axis=2).reshape(D, XG, 3 * GR)
    context = np.asarray(ctx_1024).reshape(B * XK, D)
    arrays["ctxT"] = np.concatenate([context, context[:XK]]).T
    arrays["gate_w"] = np.asarray(L0_ffn_gate_w).T
    arrays["expert_w"] = np.asarray(L0_ffn_expert_w).transpose(2, 0, 1).reshape(D, E * D)
    arrays["bias"] = bias
    arrays["comb_w"] = np.asarray(L0_ffn_combine_w).T
    arrays = {n: np.ascontiguousarray(v) for n, v in arrays.items()}

    nc = bacc.Bacc("TRN2", target_bir_lowering=False, num_devices=1)
    ins = {n: nc.dram_tensor(n + "_dram", v.shape, mybir.dt.from_np(v.dtype), kind="ExternalInput").ap() for n, v in arrays.items()}
    out = nc.dram_tensor("out_dram", (B, P, J, D), F32, kind="ExternalOutput").ap()
    post_ln_decoder(nc, ins, out)
    r = run_bass_kernel_spmd(nc, [{n + "_dram": v for n, v in arrays.items()}], core_ids=[0])
    return r.results[0]["out_dram"].transpose(0, 2, 1, 3).reshape(B, T, D)
```

```python
import concourse.bass as bass
from concourse import mybir
from contextlib import ExitStack

F32 = mybir.dt.float32
F32R = mybir.dt.float32r
BF16 = mybir.dt.bfloat16
U32 = mybir.dt.uint32
ALU = mybir.AluOpType
ACT = mybir.ActivationFunctionType
AX = mybir.AxisListType

B, T, D = 8, 256, 128
P = 128
J = T // P
RH, RV = 4, 64
RK = D // RH
VD = RH * RV
XH, XK, XD = 16, 64, 8
PAIRS = XH // 2
XG = 4
GH, GR = XH // XG, D // XG
VW = 2 * XD
E = 8
EPS = 1e-5
STAGES = 5

EVENTS = """
x_hi x_lo qk_proj v_proj g_proj rope_cos rope_sin rope_swap rotated k_spread v_kept gate_tanh gate_kept
score0 scorex score1 diag0 cross diag1
ret_out squares gated square_sums rms_eps rms_rate scaled gT gT_kept ret_proj
res1 stats1 moments1 mean1 var1_eps rate1 shift1 x1_kept x1_held x1T x1T_kept q_proj q_hi q_lo
q_picked q_spread k_masked max_scores0 max_scores1 max0 max1 max_hi max_lo maxT maxT_kept
scoresT0 scoresT1 exp0 exp1 v_placed av inv att x_proj
res2 stats2 moments2 mean2 var2_eps rate2 shift2 x2_kept x2_held x2T x2T_kept x2T_held logits logits_kept
top_max top_found top_exp top_sum top_inv top_prob weighted w_kept
y_hi y_lo w_here z0 z1 h0 h1 mixed0 mixed1 mixT mixT_kept comb
stats3 moments3 var3_eps rate3 mean3 shift3 y_kept
""".split()
ONCE = """
xT_loaded x_loaded rope_w_loaded vg_w_loaded tables_loaded ident_loaded out_w_loaded x_w_loaded ctx_loaded pick_loaded picks_made
ffn_loaded out_stored zeros_made consts_made
rope_w_hi vg_w_hi weights_made k_proj k_hi k_lo vx_proj vx_kept v_ones
expert_hi bias_lo
""".split()


def wait(engine, sem, value):
    if not isinstance(value, int) or value > 0:
        engine.wait_ge(sem, value)


def post_ln_decoder(nc, a, out):
    ctx = ExitStack()
    with ctx:
        def sb(name, shape, dt=F32):
            return ctx.enter_context(nc.sbuf_tensor(name, shape, dt))

        s = {n: ctx.enter_context(nc.semaphore(n)) for n in EVENTS + ONCE}
        mix_done = [[ctx.enter_context(nc.semaphore(f"mix{j}_{e}")) for e in range(E - 1)] for j in range(J)]

        w_qk = sb("w_qk", [D, 2, D])
        w_qk_r = sb("w_qk_r", [D, 2, 2, D], F32R)
        w_vg = sb("w_vg", [D, 2, VD])
        w_vg_r = sb("w_vg_r", [D, 2, 2, VD], F32R)
        w_ret_o = sb("w_ret_o", [P, 2, D])
        w_ret = sb("w_ret", [P, 2, D])
        norm_w = sb("norm_w", [P, 1])
        w_x = sb("w_x", [D, 3, D])
        gate_w = sb("gate_w", [D, E])
        expert_w = sb("expert_w", [D, E * D])
        expert_r = sb("expert_r", [D, 2, E * D], F32R)
        comb_w = sb("comb_w", [D, D])
        tables = sb("tables", [D, 2, 2 * T])
        squares_in = sb("squares_in", [P, 2, P])
        cos_t, sin_t = tables[:, 0, :], tables[:, 1, :]
        ident, causal = squares_in[:, 0, :], squares_in[:, 1, :]
        ident16 = sb("ident16", [P, P], BF16)
        row_pick_in = sb("row_pick_in", [D, 2, XG, 3 * GR])
        row_pick = sb("row_pick", [D, 2, XG, 3 * GR], F32R)
        head_pick = sb("head_pick", [P, PAIRS, 2, XK])
        head_mask = sb("head_mask", [3 * GR, GH])
        iota_e = sb("iota_e", [P, E])
        ones_r = sb("ones_r", [64, P], F32R)
        bias_in = sb("bias_in", [64, E * D])
        bias_r = sb("bias_r", [64, E * D], F32R)
        minus_half = sb("minus_half", [P, J * RH])
        minus_one = sb("minus_one", [P, J])
        eps_ln = sb("eps_ln", [P, J])
        eps_sum = sb("eps_sum", [P, J * RH])
        ctxT = sb("ctxT", [D, (B + 1) * XK])
        w_k3 = sb("w_k3", [D, XG, 3 * GR])
        k_parts = sb("k_parts", [3 * GR, XG, B * XK], F32R)
        v_bd = sb("v_bd", [P, B, PAIRS, VW])
        v_now = sb("v_now", [P, PAIRS, 2 * VW])
        ones_now = sb("ones_now", [P, 3 * VW])
        xT = sb("xT", [D, T])
        xT_r = sb("xT_r", [D, 2, T], F32R)
        x_in = sb("x_in", [P, J, D])
        r_cos = sb("r_cos", [D, 2 * T])
        r_sin = sb("r_sin", [D, 2 * T])
        r_swap = sb("r_swap", [D, 2 * T])
        qk = sb("qk", [D, 2, T])
        k_head = sb("k_head", [D, RH, T])
        v = sb("v", [P, J, VD])
        g_tanh = sb("g_tanh", [P, J * VD])
        gate = sb("gate", [P, J * VD])
        p_diag = sb("p_diag", [P, J, RH, P])
        p_cross = sb("p_cross", [P, RH, P])
        squares = sb("squares", [P, J * RH, RV])
        ssq = sb("ssq", [P, J * RH])
        ssq_eps = sb("ssq_eps", [P, J * RH])
        rms = sb("rms", [P, J * RH])
        u = sb("u", [P, J * RH, RV])
        og = sb("og", [P, J, 2, P])
        ogT = sb("ogT", [P, J, 2, P])
        x1 = sb("x1", [P, J, D])
        x1_all = sb("x1_all", [P, B, J, D])
        x1T = sb("x1T", [D, T])
        q_r = sb("q_r", [D, 2, T], F32R)
        ln = [dict(sum=sb(f"ln{n}_sum", [P, J, D]), stats=sb(f"ln{n}_stats", [P, J, 6]),
                   mv=sb(f"ln{n}_mv", [P, J, 2]), var=sb(f"ln{n}_var", [P, J]),
                   tick=sb(f"ln{n}_tick", [P, 1]), rate=sb(f"ln{n}_rate", [P, J]),
                   neg_mean=sb(f"ln{n}_neg_mean", [P, J]), shift=sb(f"ln{n}_shift", [P, J])) for n in range(3)]
        swap_tick = sb("swap_tick", [P, 1])
        gating_tick = sb("gating_tick", [P, 1])
        neg_max = sb("neg_max", [P, J, XH])
        max16 = sb("max16", [P, J, 2 * XH], BF16)
        q_now = sb("q_now", [P, XG, T], F32R)
        k_now = sb("k_now", [P, PAIRS, 2, XK], F32R)
        k_tick = sb("k_tick", [P, 1])
        inv = sb("inv", [D, T])
        probsT = sb("probsT", [P, PAIRS, T])
        attT = sb("attT_sb", [D, T])
        x2 = sb("x2", [P, J, D])
        x2_all = sb("x2_all", [P, B, J, D])
        x2T = sb("x2T_sb", [D, T])
        x2T_all = sb("x2T_all", [D, B, T])
        lg = sb("lg", [P, J, E])
        top = sb("top", [P, J, 8])
        top_i = sb("top_i", [P, J, 8], U32)
        top_if = sb("top_if", [P, J, 2])
        top_d = sb("top_d", [P, J, 8])
        top_e = sb("top_e", [P, J, 8])
        top_s = sb("top_s", [P, J])
        top_r = sb("top_r", [P, J])
        top_p = sb("top_p", [P, J, 2])
        hot = sb("hot", [P, J, 2, E])
        w_hot = sb("w_hot", [P, J, 2, E])
        w_all = sb("w_all", [P, B, J, E])
        w_now = sb("w_now", [P, 2, J, E])
        y_tick = sb("y_tick", [P, 1])
        y_r = sb("y_r", [D, 2, 2, T], F32R)
        h = sb("h", [P, 2, J, E, D])
        acc = sb("acc", [P, J, E, D])
        mixT_sb = sb("mixT_sb", [D, T])
        y = sb("y", [P, J, D])

        bank = ctx.enter_context(nc.psum_tensor("bank", [P, 8, 512], F32))
        H0, H1, R0, C0, XS, XA, XB = 0, 1, 2, 3, 4, 6, 7
        YB = 5, 2

        def one(t, n):
            return t[:, bass.ds(n, 1)].rearrange("p o a c -> p (o a) c")

        def halves(m):
            return bank[:, m, 0:T].rearrange("p (j d) -> p j d", j=J)

        def steady(engine, body):
            for i in range(STAGES):
                body(i)
            with engine.Fori(STAGES, B - 1) as i:
                body(i)
            for i in range(B - 1, B + STAGES - 1):
                body(i)

        def runs(i, lag):
            return not isinstance(i, int) or 0 <= i - lag < B

        def expert_steady(engine, body):
            for i in range(1, 4):
                body(i, i % 2)
            with engine.Fori(2, B // 2) as pair:
                body(2 * pair, 0)
                body(2 * pair + 1, 1)
            for i in range(B, B + 3):
                body(i, i % 2)

        block = ctx.enter_context(nc.Block())

        @block.sync
        def _(sp):
            sp.dma_start(xT[:, :], a["xT"][:, 0:T]).then_inc(s["xT_loaded"], 16)
            sp.dma_start(tables[:, :, :], a["tables"]).then_inc(s["tables_loaded"], 16)
            sp.dma_start(w_vg[:, :, :], a["w_vg"]).then_inc(s["vg_w_loaded"], 16)
            sp.dma_start(squares_in[:, :, :], a["squares"]).then_inc(s["ident_loaded"], 16)
            sp.dma_start(w_x[:, :, :], a["w_x"]).then_inc(s["x_w_loaded"], 16)
            sp.dma_start(head_mask[:, :], a["head_mask"]).then_inc(s["pick_loaded"], 16)
            sp.dma_start(row_pick_in[:, :, :, :], a["row_pick"]).then_inc(s["pick_loaded"], 16)
            sp.dma_start(w_ret_o[:, :, :], a["w_ret_o"]).then_inc(s["out_w_loaded"], 16)
            sp.dma_start(norm_w[:, :], a["norm_w"]).then_inc(s["out_w_loaded"], 16)
            sp.dma_start(x_in[:, :, :], a["x"][0]).then_inc(s["x_loaded"], 16)
            sp.dma_start(head_pick[3 * GR:P, :, :, :], a["head_pick"]).then_inc(s["pick_loaded"], 16)
            sp.dma_start(iota_e[:, :], a["iota_e"]).then_inc(s["ffn_loaded"], 16)
            sp.dma_start(gate_w[:, :], a["gate_w"]).then_inc(s["ffn_loaded"], 16)
            sp.dma_start(bias_in[:, :], a["bias"]).then_inc(s["ffn_loaded"], 16)
            sp.dma_start(expert_w[:, :], a["expert_w"]).then_inc(s["ffn_loaded"], 16)
            sp.dma_start(comb_w[:, :], a["comb_w"]).then_inc(s["ffn_loaded"], 16)
            with sp.Fori(1, B) as b:
                sp.wait_ge(s["x_lo"], b)
                sp.dma_start(xT[:, :], a["xT"][:, bass.ds(b * T, T)]).then_inc(s["xT_loaded"], 16)
                sp.wait_ge(s["res1"], b)
                sp.dma_start(x_in[:, :, :], a["x"][bass.ds(b, 1)].rearrange("o p j d -> p (o j) d"))\
                  .then_inc(s["x_loaded"], 16)
            with sp.Fori(0, B) as b:
                sp.wait_ge(s["y_kept"], b + 1)
                sp.dma_start(out[bass.ds(b, 1)].rearrange("o p j d -> p (o j) d"), y[:, :, :]).then_inc(s["out_stored"], 16)
            sp.wait_ge(s["out_stored"], 16 * B)

        @block.gpsimd
        def _(pool):
            pool.memset(k_head[:, :, :], 0.0).then_inc(s["zeros_made"], 1)
            pool.memset(v_bd[:, :, :, :], 0.0).then_inc(s["zeros_made"], 1)
            pool.memset(v_now[:, :, :], 0.0).then_inc(s["zeros_made"], 1)
            pool.memset(ones_now[:, :], 0.0).then_inc(s["zeros_made"], 1)
            pool.memset(minus_half[:, :], -0.5).then_inc(s["consts_made"], 1)
            pool.memset(minus_one[:, :], -1.0).then_inc(s["consts_made"], 1)
            pool.memset(eps_ln[:, :], EPS).then_inc(s["consts_made"], 1)
            pool.memset(eps_sum[:, :], EPS * RV).then_inc(s["consts_made"], 1)
            pool.memset(ones_r[:, :].bitcast(F32), 1.0).then_inc(s["consts_made"], 1)

            def power(var, var_eps, rate, eps, ready, eps_done, done, n):
                pool.wait_ge(ready, n + 1)
                pool.tensor_tensor(var_eps, var, eps, ALU.add).then_inc(eps_done, 1)
                pool.wait_ge(eps_done, n + 1)
                pool.tensor_tensor(rate, var_eps, minus_half[:, 0:var.shape[-1]], ALU.pow).then_inc(done, 1)

            def low_x(n):
                pool.wait_ge(s["x_hi"], n + 1)
                pool.tensor_tensor(xT_r[:, 1, :], xT[:, :], xT_r[:, 0, :].bitcast(F32), ALU.subtract).then_inc(s["x_lo"], 1)

            low_x(0)
            pool.wait_ge(s["pick_loaded"], 48)
            pool.tensor_copy(row_pick[:, :, :, :], row_pick_in[:, :, :, :]).then_inc(s["picks_made"], 1)

            def mask_keys(n):
                if isinstance(n, int) and n == 0:
                    pool.wait_ge(s["k_lo"], XG)
                else:
                    pool.wait_ge(s["scoresT0"], n)
                    pool.wait_ge(s["scoresT1"], n)
                pool.tensor_tensor(k_tick[:, :], minus_one[:, 0:1], minus_one[:, 0:1], ALU.mult)
                pool.tensor_tensor(k_now[0:3 * GR, :, :, :].rearrange("p (g n) w k -> p g (n w) k", g=XG),
                                   k_parts[:, :, bass.ds(n * XK, XK)].bitcast(F32).unsqueeze(2).broadcast_to([3 * GR, XG, GH, XK]),
                                   head_mask[:, :].unsqueeze(1).unsqueeze(3).broadcast_to([3 * GR, XG, GH, XK]), ALU.mult)\
                    .then_inc(s["k_masked"], 1)

            def rms_rate(n):
                power(ssq[:, :], ssq_eps[:, :], rms[:, :], eps_sum[:, :], s["square_sums"], s["rms_eps"], s["rms_rate"], n)

            def norm_rate(n, k):
                t = ln[k - 1]
                power(t["mv"][:, :, 1], t["var"][:, :], t["rate"][:, :], eps_ln[:, :], s[f"moments{k}"], s[f"var{k}_eps"], s[f"rate{k}"], n)
                pool.tensor_tensor(t["neg_mean"][:, :], t["mv"][:, :, 0], minus_one[:, :], ALU.mult).then_inc(s[f"mean{k}"], 1)
                pool.wait_ge(s[f"rate{k}"], n + 1)
                pool.wait_ge(s[f"mean{k}"], n + 1)
                pool.tensor_tensor(t["shift"][:, :], t["neg_mean"][:, :], t["rate"][:, :], ALU.mult).then_inc(s[f"shift{k}"], 1)

            def hold_x1(n):
                pool.wait_ge(s["x1_kept"], n + 1)
                pool.tensor_copy(one(x1_all, n), x1[:, :, :]).then_inc(s["x1_held"], 1)

            def hold_x2(n):
                pool.wait_ge(s["x2_kept"], n + 1)
                pool.tensor_copy(one(x2_all, n), x2[:, :, :]).then_inc(s["x2_held"], 1)

            def hold_x2T(n):
                pool.wait_ge(s["x2T_kept"], n + 1)
                pool.tensor_copy(x2T_all[:, bass.ds(n, 1), :].rearrange("p o t -> p (o t)"), x2T[:, :]).then_inc(s["x2T_held"], 1)

            def place_v(n):
                if isinstance(n, int) and n == 0:
                    pool.wait_ge(s["vx_kept"], 5)
                else:
                    pool.wait_ge(s["av"], n)
                pool.tensor_copy(v_now[:, :, 0:VW], v_bd[:, bass.ds(n, 1), :, :].rearrange("p o m c -> p (o m) c")).then_inc(s["v_placed"], 1)

            def load(n, parity):
                tokens = x2T_all[:, bass.ds(n, 1), :].rearrange("p o t -> p (o t)")
                pool.wait_ge(s["x2T_held"], n + 1)
                wait(pool, s["z1"], n - 1)
                pool.tensor_copy(y_r[:, parity, 0, :], tokens).then_inc(s["y_hi"], 1)
                pool.wait_ge(s["y_hi"], n + 1)
                pool.tensor_tensor(y_tick[:, :], minus_one[:, 0:1], minus_one[:, 0:1], ALU.mult)
                pool.tensor_tensor(y_r[:, parity, 1, :], tokens, y_r[:, parity, 0, :].bitcast(F32), ALU.subtract).then_inc(s["y_lo"], 1)
                pool.wait_ge(s["w_kept"], n + 1)
                wait(pool, s["mixed1"], n - 1)
                pool.tensor_copy(w_now[:, parity, :, :], one(w_all, n)).then_inc(s["w_here"], 1)

            def step(i):
                if runs(i, 2):
                    hold_x1(i - 2)
                if runs(i, 4):
                    norm_rate(i - 4, 2)
                if runs(i, 2):
                    mask_keys(i - 2)
                if runs(i, 1):
                    norm_rate(i - 1, 1)
                if runs(i, 4):
                    hold_x2T(i - 4)
                if runs(i, 2):
                    place_v(i - 2)
                if runs(i, -1):
                    low_x(i + 1)
                if runs(i, 4):
                    hold_x2(i - 4)
                if runs(i, 0):
                    rms_rate(i)
                if isinstance(i, int) and i == B:
                    load(0, 0)

            pool.wait_ge(s["consts_made"], 5)
            steady(pool, step)

            def expert_step(i, parity):
                if runs(i, 0):
                    load(i, parity)
                if runs(i, 3):
                    wait(pool, s["y_kept"], i - 3)
                    norm_rate(i - 3, 3)

            pool.wait_ge(s["x2T_held"], B)
            expert_steady(pool, expert_step)

        @block.scalar
        def _(act):
            act.dma_start(w_qk[:, :, :], a["w_qk"]).then_inc(s["rope_w_loaded"], 16)
            act.dma_start(ctxT[:, :], a["ctxT"]).then_inc(s["ctx_loaded"], 16)
            act.dma_start(w_k3[:, :, :], a["w_k3"]).then_inc(s["ctx_loaded"], 16)
            act.preload_act_table_set("exp_and_others")

            def split_x(n):
                act.wait_ge(s["xT_loaded"], 16 * n + 16)
                wait(act, s["g_proj"], n)
                act.activation(xT_r[:, 0, :], xT[:, :], ACT.Copy).then_inc(s["x_hi"], 1)

            split_x(0)
            act.wait_ge(s["rope_w_loaded"], 16)
            act.activation(w_qk_r[:, 0, :, :], w_qk[:, :, :], ACT.Copy).then_inc(s["rope_w_hi"], 1)
            act.wait_ge(s["vg_w_loaded"], 16)
            act.activation(w_vg_r[:, 0, :, :], w_vg[:, :, :], ACT.Copy).then_inc(s["vg_w_hi"], 1)

            def normalise(n, k, dst, src):
                act.wait_ge(s[f"rate{k}"], n + 1)
                act.wait_ge(s[f"shift{k}"], n + 1)
                t = ln[k - 1]
                for j in range(J):
                    last = act.activation(dst[:, j, :], src[:, j, :], ACT.Identity, bias=t["shift"][:, j:j + 1], scale=t["rate"][:, j:j + 1])
                last.then_inc(s[("x1_kept", "x2_kept", "y_kept")[k - 1]], 1)

            def norm1_end(n):
                wait(act, s["x1T"], n)
                wait(act, s["x1_held"], n)
                normalise(n, 1, x1, ln[0]["sum"])

            def norm2_end(n):
                wait(act, s["x2T"], n)
                wait(act, s["x2_held"], n)
                normalise(n, 2, x2, ln[1]["sum"])

            def scale_rms(n):
                act.wait_ge(s["rms_rate"], n + 1)
                act.wait_ge(s["gated"], n + 1)
                wait(act, s["gT"], n)
                og_heads = og[:, :, :, :].rearrange("p j n (m c) -> p (j n m) c", c=RV)
                for m in range(J * RH):
                    last = act.activation(og_heads[:, m, :], u[:, m, :], ACT.Copy, scale=rms[:, m:m + 1])
                last.then_inc(s["scaled"], 1)

            def keep_v(n):
                act.wait_ge(s["v_proj"], n + 1)
                wait(act, s["ret_out"], n)
                act.activation(v[:, :, :], bank[:, H1, :].rearrange("p (j n) -> p j n", j=J), ACT.Copy).then_inc(s["v_kept"], 1)

            def max_out(n):
                act.wait_ge(s["maxT"], n + 1)
                wait(act, s["scoresT0"], n)
                wait(act, s["scoresT1"], n)
                act.activation(q_now[3 * GR:P, :, :], bank[3 * GR:P, XS, 0:T // 2].bitcast(BF16).unsqueeze(1).broadcast_to([2 * XH, XG, T]),
                               ACT.Copy).then_inc(s["maxT_kept"], 1)

            def square(n):
                act.wait_ge(s["ret_out"], n + 1)
                wait(act, s["square_sums"], n)
                act.activation(squares[:, :, :], bank[:, R0, :].rearrange("p (n c) -> p n c", c=RV), ACT.Square).then_inc(s["squares"], 1)

            def exponent(n, half):
                act.wait_ge(s[f"scoresT{half}"], n + 1)
                wait(act, s["av"], n)
                m = (XA, XS)[half]
                act.activation(probsT[:, 4 * half:4 * half + 4, :], bank[:, m:m + 2, :].rearrange("p n (m t) -> p (n m) t", t=T),
                               ACT.Exp).then_inc(s[f"exp{half}"], 1)

            def spread_k(n):
                act.wait_ge(s["rotated"], n + 1)
                wait(act, s["score1"], n)
                wait(act, s["scorex"], n)
                wait(act, s["k_spread"], n)
                if isinstance(n, int) and n == 0:
                    act.wait_ge(s["zeros_made"], 1)
                for m in range(RH):
                    r = slice(RK * m, RK * m + RK)
                    last = act.activation(k_head[r, m, :], qk[r, 1, :], ACT.Copy)
                last.then_inc(s["k_spread"], 1)

            def tanh(n):
                act.wait_ge(s["g_proj"], n + 1)
                wait(act, s["gate_kept"], n)
                act.activation(g_tanh[:, :], bank[:, H0, :], ACT.Tanh, scale=0.5).then_inc(s["gate_tanh"], 1)

            def g_out(n):
                act.wait_ge(s["gT"], n + 1)
                wait(act, s["ret_proj"], n)
                act.activation(ogT[:, :, :, :], bank[:, R0, :].rearrange("p (j n c) -> p j n c", j=J, n=2), ACT.Copy).then_inc(s["gT_kept"], 1)

            def cross_out(n):
                act.wait_ge(s["scorex"], n + 1)
                wait(act, s["ret_out"], n)
                act.activation(p_cross[:, :, :], bank[:, H0, :].rearrange("p (n c) -> p n c", c=P), ACT.Copy).then_inc(s["cross"], 1)

            def x2_out(n):
                act.wait_ge(s["x2T"], n + 1)
                wait(act, s["logits"], n)
                wait(act, s["x2T_held"], n)
                act.activation(x2T[:, :], bank[:, C0, 0:T], ACT.Copy).then_inc(s["x2T_kept"], 1)

            def logits_out(n):
                act.wait_ge(s["logits"], n + 1)
                wait(act, s["top_found"], n)
                act.activation(lg[:, :, :], bank[:, C0, 0:J * E].rearrange("p (j e) -> p j e", j=J), ACT.Copy).then_inc(s["logits_kept"], 1)

            def top_exp(n):
                act.wait_ge(s["top_found"], n + 1)
                wait(act, s["top_prob"], n)
                act.activation(top_e[:, :, :], top_d[:, :, :], ACT.Exp).then_inc(s["top_exp"], 1)

            def x1_out(n):
                act.wait_ge(s["x1T"], n + 1)
                wait(act, s["q_proj"], n)
                act.activation(x1T[:, :], bank[:, C0, 0:T], ACT.Copy).then_inc(s["x1T_kept"], 1)

            def query_hi(n):
                act.wait_ge(s["q_proj"], n + 1)
                wait(act, s["q_picked"], n)
                act.activation(q_r[:, 0, :], bank[:, C0, 0:T], ACT.Copy, scale=XD ** -0.5).then_inc(s["q_hi"], 1)

            def spread_q(n):
                act.wait_ge(s["q_picked"], n + 1)
                wait(act, s["scoresT0"], n)
                wait(act, s["scoresT1"], n)
                act.activation(q_now[0:3 * GR, :, :], bank[0:3 * GR, XA:XA + 2, :].rearrange("p n (m t) -> p (n m) t", t=T),
                               ACT.Copy).then_inc(s["q_spread"], 1)

            def keep_keys():
                for g in range(XG):
                    act.wait_ge(s["k_proj"], g + 1)
                    act.activation(k_parts[:, g, :], bank[0:3 * GR, R0 + g, :], ACT.Copy).then_inc(s["k_hi"], 1)

            def keep_values():
                act.wait_ge(s["zeros_made"], 4)
                act.wait_ge(s["vx_proj"], B)
                for m in range(2):
                    for half in range(2):
                        lo = XK * half
                        src = bank[lo:lo + XK, XA + m, :].rearrange("p (b n w c) -> p b n w c", n=PAIRS, w=2, c=XD)[:, :, :, half, :]
                        first = 4 * m + half
                        count = min(4, B - first)
                        act.activation(v_bd[lo:lo + XK, first:first + count, :, XD * half:XD * half + XD], src[:, 0:count], ACT.Copy)\
                           .then_inc(s["vx_kept"], 1)
                act.activation(v_bd[XK:P, 0:1, :, XD:2 * XD], src[:, 3:4], ACT.Copy).then_inc(s["vx_kept"], 1)

            def step(i):
                if runs(i, 3):
                    exponent(i - 3, 1)
                if runs(i, 0):
                    keep_v(i)
                if runs(i, 2):
                    query_hi(i - 2)
                if runs(i, 1):
                    scale_rms(i - 1)
                if runs(i, 0):
                    spread_k(i)
                if runs(i, 1):
                    g_out(i - 1)
                if runs(i, 0):
                    tanh(i)
                if isinstance(i, int) and i == 0:
                    keep_keys()
                if runs(i, 4):
                    norm2_end(i - 4)
                if runs(i, 2):
                    spread_q(i - 2)
                if runs(i, 4):
                    x2_out(i - 4)
                if runs(i, 0):
                    cross_out(i)
                if runs(i, 1):
                    norm1_end(i - 1)
                if runs(i, 4):
                    logits_out(i - 4)
                if runs(i, -1):
                    split_x(i + 1)
                if runs(i, 2):
                    max_out(i - 2)
                if runs(i, 0):
                    square(i)
                if runs(i, 4):
                    top_exp(i - 4)
                if runs(i, 1):
                    x1_out(i - 1)
                if runs(i, 2):
                    exponent(i - 2, 0)
                if isinstance(i, int) and i == 0:
                    keep_values()

            steady(act, step)

            def silu(n, parity, j):
                act.wait_ge(s[f"z{j}"], n + 1)
                wait(act, s[f"mixed{j}"], n - 1)
                act.activation(h[:, parity, j, :, :], bank[:, (H0, XA)[j]:(H0, XA)[j] + 2, :].rearrange("p n (e d) -> p (n e) d", d=D), ACT.Silu)\
                   .then_inc(s[f"h{j}"], 1)

            def mixed_out(n):
                act.wait_ge(s["mixT"], n + 1)
                wait(act, s["comb"], n)
                act.activation(mixT_sb[:, :], bank[:, 4, 0:T], ACT.Copy).then_inc(s["mixT_kept"], 1)

            def expert_step(i, parity):
                if runs(i, 2):
                    mixed_out(i - 2)
                if runs(i, 0):
                    silu(i, parity, 0)
                    silu(i, parity, 1)
                if runs(i, 3):
                    wait(act, s["out_stored"], 16 * (i - 3))
                    normalise(i - 3, 3, y, halves(YB[1 - parity]))

            expert_step(0, 0)
            expert_steady(act, expert_step)

        @block.vector
        def _(dve):
            def layer_norm(n, k, add_a, add_b):
                t = ln[k - 1]
                wait(dve, s[("x1_kept", "x2_kept")[k - 1]], n)
                dve.tensor_tensor(t["sum"][:, :, :], add_a, add_b, ALU.add).then_inc(s[f"res{k}"], 1)
                dve.wait_ge(s[f"res{k}"], n + 1)
                moments(n, k, t["sum"])

            def moments(n, k, tokens):
                t = ln[k - 1]
                for j in range(J):
                    last = dve.bn_stats(t["stats"][:, j, :], tokens[:, j, :])
                last.then_inc(s[f"stats{k}"], 1)
                dve.wait_ge(s[f"stats{k}"], n + 1)
                dve.memset(t["tick"][:, :], 0.0)
                for j in range(J):
                    last = dve.bn_aggr(t["mv"][:, j, :], t["stats"][:, j, :])
                last.then_inc(s[f"moments{k}"], 1)

            def rope_multiply(n):
                dve.wait_ge(s["qk_proj"], n + 1)
                dve.tensor_tensor(r_sin[:, :], bank[:, H0, :], sin_t, ALU.mult).then_inc(s["rope_sin"], 1)
                dve.tensor_tensor(r_cos[:, :], bank[:, H0, :], cos_t, ALU.mult).then_inc(s["rope_cos"], 1)

            def rope_swap(n):
                dve.wait_ge(s["rope_sin"], n + 1)
                dve.memset(swap_tick[:, :], 0.0)
                dve.stream_shuffle(r_swap[:, :], r_sin[:, :], [(p + RK // 2) % RK for p in range(32)]).then_inc(s["rope_swap"], 1)

            def rope_add(n):
                dve.wait_ge(s["rope_cos"], n + 1)
                dve.wait_ge(s["rope_swap"], n + 1)
                wait(dve, s["score1"], n)
                wait(dve, s["scorex"], n)
                dve.tensor_tensor(qk[:, :, :].rearrange("p a t -> p (a t)"), r_cos[:, :], r_swap[:, :], ALU.add).then_inc(s["rotated"], 1)

            def gates(n):
                dve.wait_ge(s["gate_tanh"], n + 1)
                wait(dve, s["gated"], n)
                dve.scalar_tensor_tensor(gate[:, :], g_tanh[:, :], 1.0, bank[:, H0, :], ALU.add, ALU.mult).then_inc(s["gate_kept"], 1)

            def diagonal(n, k):
                dve.wait_ge(s[f"score{k}"], n + 1)
                wait(dve, s["ret_out"], n)
                dve.tensor_tensor(p_diag[:, k, :, :], bank[:, H1, :].rearrange("p (n c) -> p n c", c=P),
                                  causal.unsqueeze(1).broadcast_to([P, RH, P]), ALU.mult).then_inc(s[f"diag{k}"], 1)

            def gated(n):
                dve.wait_ge(s["squares"], n + 1)
                dve.tensor_tensor(u[:, :, :], gate[:, :].rearrange("p (n c) -> p n c", c=RV),
                                  bank[:, R0, :].rearrange("p (n c) -> p n c", c=RV), ALU.mult).then_inc(s["gated"], 1)

            def square_sums(n):
                dve.wait_ge(s["squares"], n + 1)
                wait(dve, s["rms_eps"], n)
                dve.tensor_reduce(ssq[:, :], squares[:, :, :], AX.X, ALU.add).then_inc(s["square_sums"], 1)

            def norm1(n):
                dve.wait_ge(s["ret_proj"], n + 1)
                dve.wait_ge(s["x_loaded"], 16 * n + 16)
                layer_norm(n, 1, halves(R0), x_in[:, :, :])

            def query_lo(n):
                dve.wait_ge(s["q_hi"], n + 1)
                dve.scalar_tensor_tensor(q_r[:, 1, :], bank[:, C0, 0:T], XD ** -0.5, q_r[:, 0, :].bitcast(F32),
                                         ALU.mult, ALU.subtract).then_inc(s["q_lo"], 1)

            def maximum(n, j):
                dve.wait_ge(s[f"max_scores{j}"], n + 1)
                wait(dve, s["max_lo"], n)
                m = (XS, XA)[j]
                dve.tensor_reduce(neg_max[:, j, :], bank[:, m:m + 2, :].rearrange("p n (h k) -> p (n h) k", k=XK),
                                  AX.X, ALU.max, negate=True).then_inc(s[f"max{j}"], 1)

            def max_hi(n):
                dve.wait_ge(s["max0"], n + 1)
                dve.wait_ge(s["max1"], n + 1)
                wait(dve, s["maxT"], n)
                dve.tensor_copy(max16[:, :, 0:XH], neg_max[:, :, :]).then_inc(s["max_hi"], 1)

            def max_lo(n):
                dve.wait_ge(s["max_hi"], n + 1)
                dve.tensor_tensor(max16[:, :, XH:2 * XH], neg_max[:, :, :], max16[:, :, 0:XH], ALU.subtract).then_inc(s["max_lo"], 1)

            def invert(n):
                dve.wait_ge(s["av"], n + 1)
                wait(dve, s["att"], n)
                dve.reciprocal(inv[:, :], bank[:, XS, T:2 * T]).then_inc(s["inv"], 1)

            def attended(n):
                dve.wait_ge(s["inv"], n + 1)
                wait(dve, s["x_proj"], n)
                dve.tensor_tensor(attT[:, :], bank[:, XS, 0:T], inv[:, :], ALU.mult).then_inc(s["att"], 1)

            def norm2(n):
                dve.wait_ge(s["x_proj"], n + 1)
                dve.wait_ge(s["x1_held"], n + 1)
                layer_norm(n, 2, halves(C0), one(x1_all, n))

            def gating_1(n):
                dve.wait_ge(s["logits_kept"], n + 1)
                wait(dve, s["top_inv"], n)
                dve.memset(gating_tick[:, :], 0.0)
                for j in range(J):
                    last = dve.max(top[:, j, :], lg[:, j, :])
                last.then_inc(s["top_max"], 1)

            def gating_2(n):
                dve.wait_ge(s["top_max"], n + 1)
                wait(dve, s["top_exp"], n)
                dve.tensor_tensor(top_d[:, :, :], top[:, :, :], top[:, :, 0:1].broadcast_to([P, J, 8]), ALU.subtract)
                for j in range(J):
                    last = dve.max_index(top_i[:, j, :], top[:, j, :], lg[:, j, :])
                last.then_inc(s["top_found"], 1)

            def gating_3(n):
                dve.wait_ge(s["top_found"], n + 1)
                dve.tensor_copy(top_if[:, :, :], top_i[:, :, 0:2])
                dve.wait_ge(s["top_exp"], n + 1)
                dve.tensor_reduce(top_s[:, :], top_e[:, :, :], AX.X, ALU.add).then_inc(s["top_sum"], 1)

            def gating_4(n):
                dve.wait_ge(s["top_sum"], n + 1)
                dve.tensor_tensor(hot[:, :, :, :], iota_e[:, :].unsqueeze(1).unsqueeze(1).broadcast_to([P, J, 2, E]),
                                  top_if[:, :, :].unsqueeze(3).broadcast_to([P, J, 2, E]), ALU.is_equal)
                dve.reciprocal(top_r[:, :], top_s[:, :]).then_inc(s["top_inv"], 1)

            def gating_5(n):
                dve.wait_ge(s["top_inv"], n + 1)
                dve.tensor_tensor(top_p[:, :, :], top_e[:, :, 0:2], top_r[:, :].unsqueeze(2).broadcast_to([P, J, 2]), ALU.mult).then_inc(s["top_prob"], 1)

            def gating_6(n):
                dve.wait_ge(s["top_prob"], n + 1)
                dve.tensor_tensor(w_hot[:, :, :, :], hot[:, :, :, :], top_p[:, :, :].unsqueeze(3).broadcast_to([P, J, 2, E]), ALU.mult).then_inc(s["weighted"], 1)

            def gating_7(n):
                dve.wait_ge(s["weighted"], n + 1)
                dve.tensor_tensor(one(w_all, n), w_hot[:, :, 0, :], w_hot[:, :, 1, :], ALU.add).then_inc(s["w_kept"], 1)

            def step(i):
                if runs(i, 0):
                    rope_multiply(i)
                    rope_swap(i)
                    rope_add(i)
                if runs(i, 2):
                    query_lo(i - 2)
                if runs(i, 3):
                    invert(i - 3)
                if runs(i, 0):
                    gates(i)
                if runs(i, 3):
                    attended(i - 3)
                if runs(i, 0):
                    diagonal(i, 0)
                if isinstance(i, int) and i == 0:
                    for g in range(XG):
                        dve.wait_ge(s["k_hi"], g + 1)
                        low = slice(2 * GR, 3 * GR)
                        dve.tensor_tensor(k_parts[low, g, :], bank[low, R0 + g, 0:B * XK], k_parts[low, g, :].bitcast(F32), ALU.subtract).then_inc(s["k_lo"], 1)
                if runs(i, 1):
                    norm1(i - 1)
                if runs(i, 0):
                    diagonal(i, 1)
                if runs(i, 2):
                    maximum(i - 2, 0)
                    maximum(i - 2, 1)
                    max_hi(i - 2)
                    max_lo(i - 2)
                if runs(i, 4):
                    gating_1(i - 4)
                    gating_2(i - 4)
                if runs(i, 3):
                    norm2(i - 3)
                if runs(i, 0):
                    square_sums(i)
                if runs(i, 4):
                    gating_3(i - 4)
                    gating_4(i - 4)
                if runs(i, 0):
                    gated(i)
                if runs(i, 4):
                    gating_5(i - 4)
                    gating_6(i - 4)
                    gating_7(i - 4)
                if isinstance(i, int) and i == 0:
                    for half in range(2):
                        dve.memset(ones_now[XK * half:XK * half + XK, VW + XD * half:VW + XD * half + XD], 1.0).then_inc(s["v_ones"], 1)
                if isinstance(i, int) and i == 1:
                    dve.wait_ge(s["pick_loaded"], 48)
                    dve.tensor_copy(k_now[3 * GR:P, :, :, :], head_pick[3 * GR:P, :, :, :]).then_inc(s["picks_made"], 1)
                if isinstance(i, int) and i == B:
                    dve.wait_ge(s["ffn_loaded"], 80)
                    dve.tensor_copy(bias_r[:, :], bias_in[:, :])
                    dve.tensor_copy(expert_r[:, 0, :], expert_w[:, :]).then_inc(s["expert_hi"], 1)
                    dve.wait_ge(s["expert_hi"], 1)
                    dve.tensor_tensor(expert_r[:, 1, :], expert_w[:, :], expert_r[:, 0, :].bitcast(F32), ALU.subtract)
                    dve.tensor_tensor(bias_r[32:64, :], bias_in[32:64, :], bias_r[32:64, :].bitcast(F32), ALU.subtract).then_inc(s["bias_lo"], 1)

            dve.wait_ge(s["rope_w_hi"], 1)
            dve.tensor_tensor(w_qk_r[:, 1, :, :], w_qk[:, :, :], w_qk_r[:, 0, :, :].bitcast(F32), ALU.subtract).then_inc(s["weights_made"], 1)
            dve.wait_ge(s["vg_w_hi"], 1)
            dve.tensor_tensor(w_vg_r[:, 1, :, :], w_vg[:, :, :], w_vg_r[:, 0, :, :].bitcast(F32), ALU.subtract).then_inc(s["weights_made"], 1)
            dve.wait_ge(s["ident_loaded"], 16)
            dve.tensor_copy(ident16[:, :], ident).then_inc(s["weights_made"], 1)
            dve.wait_ge(s["out_w_loaded"], 32)
            dve.tensor_scalar(w_ret[:, :, :], w_ret_o[:, :, :], norm_w[:, 0:1], 0.5 * RV ** 0.5, ALU.mult, ALU.mult).then_inc(s["weights_made"], 1)
            dve.wait_ge(s["tables_loaded"], 16)
            steady(dve, step)

            def mix(n, parity):
                dve.wait_ge(s["w_here"], n + 1)
                dve.wait_ge(s["h0"], n + 1)
                dve.wait_ge(s["h1"], n + 1)
                wait(dve, s["mixT"], n)
                for e in range(E):
                    for j in range(J):
                        w = w_now[:, parity, j, e:e + 1]
                        if e == 0:
                            dve.tensor_scalar(acc[:, j, 0, :], h[:, parity, j, 0, :], w, None, ALU.mult).then_inc(mix_done[j][0], 1)
                        else:
                            dve.wait_ge(mix_done[j][e - 1], n + 1)
                            dve.scalar_tensor_tensor(acc[:, j, e, :], h[:, parity, j, e, :], w, acc[:, j, e - 1, :], ALU.mult, ALU.add)\
                               .then_inc(mix_done[j][e] if e < E - 1 else s[f"mixed{j}"], 1)

            def expert_step(i, parity):
                if runs(i, 2):
                    mix(i - 2, parity)
                if runs(i, 3):
                    dve.wait_ge(s["comb"], i - 2)
                    wait(dve, s["shift3"], i - 3)
                    moments(i - 3, 3, halves(YB[1 - parity]))

            expert_steady(dve, expert_step)

        @block.tensor
        def _(pe):
            def mm(o, l, r, start=True, stop=True, **k):
                return pe.matmul(o, l, r, start=start, stop=stop, **k)

            def mm3(o, left, right):
                mm(o, left(0), right(0), stop=False)
                mm(o, left(0), right(1), start=False, stop=False)
                return mm(o, left(1), right(0), start=False)

            def project_qk(n):
                pe.wait_ge(s["x_hi"], n + 1)
                pe.wait_ge(s["x_lo"], n + 1)
                wait(pe, s["cross"], n)
                for m in range(2):
                    last = mm3(bank[:, H0, m * T:(m + 1) * T], lambda k: w_qk_r[:, k, m, :], lambda k: xT_r[:, k, :])
                last.then_inc(s["qk_proj"], 1)

            def project_vg(n, m):
                if m == 0:
                    wait(pe, s["diag1"], n)
                else:
                    pe.wait_ge(s["rope_cos"], n + 1)
                for j in range(J):
                    last = mm3(bank[:, (H1, H0)[m], j * VD:(j + 1) * VD], lambda k: xT_r[:, k, j * P:(j + 1) * P],
                               lambda k: w_vg_r[:, k, m, :])
                last.then_inc(s[("v_proj", "g_proj")[m]], 1)

            def ret_scores(n, k):
                sc, tq, name = ((0, 0, "score0"), (1, 1, "score1"), (0, 1, "scorex"))[k]
                pe.wait_ge(s["k_spread"], n + 1)
                if k == 0:
                    pe.wait_ge(s["v_kept"], n + 1)
                elif k == 2:
                    pe.wait_ge(s["gate_kept"], n + 1)
                else:
                    pe.wait_ge(s["diag0"], n + 1)
                for m in range(RH):
                    last = mm(bank[:, H0 if k == 2 else H1, m * P:(m + 1) * P], k_head[:, m, sc * P:(sc + 1) * P],
                              qk[:, 0, tq * P:(tq + 1) * P])
                last.then_inc(s[name], 1)

            def ret_out(n):
                if isinstance(n, int) and n == 0:
                    pe.wait_ge(s["k_lo"], XG)
                pe.wait_ge(s["diag0"], n + 1)
                pe.wait_ge(s["diag1"], n + 1)
                pe.wait_ge(s["cross"], n + 1)
                pe.wait_ge(s["v_kept"], n + 1)
                wait(pe, s["res1"], n)
                for m in range(RH):
                    vm = slice(m * RV, (m + 1) * RV)
                    o = bank[:, R0, m * RV:(m + 1) * RV]
                    mm(o, p_diag[:, 0, m, :], v[:, 0, vm])
                    o = bank[:, R0, VD + m * RV:VD + (m + 1) * RV]
                    mm(o, p_cross[:, m, :], v[:, 0, vm], stop=False)
                    last = mm(o, p_diag[:, 1, m, :], v[:, 1, vm], start=False)
                last.then_inc(s["ret_out"], 1)

            def g_T(n):
                pe.wait_ge(s["scaled"], n + 1)
                for k in range(2 * J):
                    last = pe.transpose(bank[:, R0, k * P:(k + 1) * P], og[:, k // 2, k % 2, :], ident)
                last.then_inc(s["gT"], 1)

            def ret_proj(n):
                pe.wait_ge(s["gT_kept"], n + 1)
                for j in range(J):
                    for m in range(2):
                        last = mm(bank[:, R0, j * P:(j + 1) * P], ogT[:, j, m, :], w_ret[:, m, :], start=m == 0, stop=m == 1)
                last.then_inc(s["ret_proj"], 1)

            def x1_T(n):
                pe.wait_ge(s["x1_kept"], n + 1)
                wait(pe, s["res2"], n - 1)
                for j in range(J):
                    last = pe.transpose(bank[:, C0, j * P:(j + 1) * P], x1[:, j, :], ident)
                last.then_inc(s["x1T"], 1)

            def query(n):
                pe.wait_ge(s["x1T_kept"], n + 1)
                mm(bank[:, C0, 0:T], w_x[:, 0, :], x1T[:, :]).then_inc(s["q_proj"], 1)

            def pick_q(n):
                if isinstance(n, int) and n == 0:
                    pe.wait_ge(s["picks_made"], 2)
                    pe.wait_ge(s["vx_kept"], 5)
                pe.wait_ge(s["q_lo"], n + 1)
                wait(pe, s["exp0"], n)
                for g in range(XG):
                    o = bank[0:3 * GR, XA + g // 2, (g % 2) * T:(g % 2) * T + T]
                    mm(o, row_pick[:, 0, g, :], q_r[:, 0, :], stop=False)
                    last = mm(o, row_pick[:, 1, g, :], q_r[:, 1, :], start=False)
                last.then_inc(s["q_picked"], 1)

            def max_scores(n, j):
                if j == 0:
                    pe.wait_ge(s["q_spread"], n + 1)
                    pe.wait_ge(s["k_masked"], n + 1)
                    wait(pe, s["att"], n)
                for g in range(XG):
                    last = mm(bank[:, (XS, XA)[j] + g // 2, (g % 2) * T:(g % 2) * T + T], q_now[0:3 * GR, g, j * P:(j + 1) * P],
                              k_now[0:3 * GR, 2 * g:2 * g + 2, :, :].rearrange("p n w k -> p (n w k)"))
                last.then_inc(s[f"max_scores{j}"], 1)

            def max_T(n):
                pe.wait_ge(s["max_lo"], n + 1)
                for j in range(J):
                    last = pe.transpose(bank[3 * GR:P, XS, j * P // 2:(j + 1) * P // 2].bitcast(BF16), max16[:, j, :], ident16[:, :],
                                        tile_position=(0, 3 * GR))
                last.then_inc(s["maxT"], 1)

            def scores_T(n, half):
                pe.wait_ge(s["maxT_kept"], n + 1)
                for m in range(PAIRS // 2):
                    pair = PAIRS // 2 * half + m
                    last = mm(bank[:, (XA, XS)[half] + m // 2, (m % 2) * T:(m % 2) * T + T], k_now[:, pair, :, :].rearrange("p w k -> p (w k)"),
                              q_now[:, pair // 2, :])
                last.then_inc(s[f"scoresT{half}"], 1)

            def values(n):
                pe.wait_ge(s["exp0"], n + 1)
                pe.wait_ge(s["exp1"], n + 1)
                pe.wait_ge(s["v_placed"], n + 1)
                if isinstance(n, int) and n == 0:
                    pe.wait_ge(s["v_ones"], 2)
                v_cols = v_now[:, :, :].rearrange("p m c -> p (m c)")
                for what in range(2):
                    for odd in range(2):
                        for k in range(PAIRS // 2):
                            m = 2 * k + odd
                            at = 2 * VW * m - VW * odd
                            left = ones_now[:, VW - VW * odd:3 * VW - VW * odd] if what else v_cols[:, at:at + 2 * VW]
                            last = mm(bank[32 * k:32 * k + 32, XS, T * what:T * what + T], left, probsT[:, m, :],
                                      start=odd == 0, stop=odd == 1, tile_position=(0, 32 * k))
                last.then_inc(s["av"], 1)

            def x_proj(n):
                pe.wait_ge(s["att"], n + 1)
                wait(pe, s["logits_kept"], n)
                for j in range(J):
                    last = mm(bank[:, C0, j * P:(j + 1) * P], attT[:, j * P:(j + 1) * P], w_x[:, 2, :])
                last.then_inc(s["x_proj"], 1)

            def x2_T(n):
                pe.wait_ge(s["x2_kept"], n + 1)
                wait(pe, s["q_lo"], min(n + 3, B) if isinstance(n, int) else n + 3)
                for j in range(J):
                    last = pe.transpose(bank[:, C0, j * P:(j + 1) * P], x2[:, j, :], ident)
                last.then_inc(s["x2T"], 1)

            def logits(n):
                pe.wait_ge(s["x2T_kept"], n + 1)
                for j in range(J):
                    last = mm(bank[:, C0, j * E:(j + 1) * E], x2T[:, j * P:(j + 1) * P], gate_w[:, :])
                last.then_inc(s["logits"], 1)

            def context_keys():
                pe.wait_ge(s["ctx_loaded"], 32)
                for g in range(XG):
                    mm(bank[0:3 * GR, R0 + g, :], w_k3[:, g, :], ctxT[:, 0:B * XK]).then_inc(s["k_proj"], 1)

            def context_values():
                pe.wait_ge(s["x_w_loaded"], 16)
                for b in range(B):
                    mm(bank[:, XA + b // 4, b % 4 * D:b % 4 * D + D], ctxT[:, b * XK:(b + 2) * XK], w_x[:, 1, :]).then_inc(s["vx_proj"], 1)

            def experts(n, parity, j):
                pe.wait_ge(s["y_hi"], n + 1)
                pe.wait_ge(s["y_lo"], n + 1)
                wait(pe, s[f"h{j}"], n)
                for m in range(2):
                    o = bank[:, (H0, XA)[j] + m, :]
                    cols = slice(m * 512, (m + 1) * 512)
                    hi, lo = (y_r[:, parity, part, j * P:(j + 1) * P] for part in range(2))
                    mm(o, hi, expert_r[:, 0, cols], stop=False)
                    mm(o, hi, expert_r[:, 1, cols], start=False, stop=False)
                    mm(o, lo, expert_r[:, 0, cols], start=False, stop=False)
                    last = mm(o, ones_r[:, :], bias_r[:, cols], start=False)
                last.then_inc(s[f"z{j}"], 1)

            def step(i):
                if runs(i, 0):
                    project_qk(i)
                if isinstance(i, int) and i == 0:
                    context_keys()
                    pe.wait_ge(s["weights_made"], 4)
                if runs(i, 0):
                    project_vg(i, 0)
                if runs(i, 2):
                    query(i - 2)
                if runs(i, 3):
                    values(i - 3)
                if runs(i, 0):
                    project_vg(i, 1)
                if isinstance(i, int) and i == 0:
                    context_values()
                if runs(i, 1):
                    g_T(i - 1)
                if runs(i, 2):
                    pick_q(i - 2)
                if runs(i, 0):
                    ret_scores(i, 0)
                if runs(i, 1):
                    ret_proj(i - 1)
                if runs(i, 0):
                    ret_scores(i, 2)
                if runs(i, 4):
                    x2_T(i - 4)
                if runs(i, 0):
                    ret_scores(i, 1)
                if runs(i, 2):
                    max_scores(i - 2, 0)
                if runs(i, 4):
                    logits(i - 4)
                if runs(i, 2):
                    max_scores(i - 2, 1)
                if runs(i, 0):
                    ret_out(i)
                if runs(i, 2):
                    max_T(i - 2)
                if runs(i, 3):
                    x_proj(i - 3)
                if runs(i, 1):
                    x1_T(i - 1)
                if runs(i, 2):
                    scores_T(i - 2, 0)
                    scores_T(i - 2, 1)
                if isinstance(i, int) and i == B + 2:
                    pe.wait_ge(s["bias_lo"], 1)
                    pe.wait_ge(s["exp0"], B)
                    pe.wait_ge(s["cross"], B)
                    pe.wait_ge(s["diag1"], B)
                    for j in range(J):
                        experts(0, 0, j)

            pe.wait_ge(s["weights_made"], 1)
            steady(pe, step)

            def mixed_T(n):
                pe.wait_ge(s["mixed0"], n + 1)
                pe.wait_ge(s["mixed1"], n + 1)
                wait(pe, s["mixT_kept"], n)
                for j in range(J):
                    last = pe.transpose(bank[:, 4, j * P:(j + 1) * P], acc[:, j, E - 1, :], ident)
                last.then_inc(s["mixT"], 1)

            def combine(n, parity):
                pe.wait_ge(s["mixT_kept"], n + 1)
                mm(bank[:, YB[parity], 0:T], ident, x2_all[:, bass.ds(n, 1), :, :].rearrange("p o j d -> p (o j d)"), stop=False, skip_group_check=True)
                for j in range(J):
                    last = mm(bank[:, YB[parity], j * P:(j + 1) * P], mixT_sb[:, j * P:(j + 1) * P], comb_w[:, :], start=False, skip_group_check=True)
                last.then_inc(s["comb"], 1)

            def expert_step(i, parity):
                if runs(i, 3):
                    mixed_T(i - 3)
                first = isinstance(i, int) and i == 1
                if runs(i, 1) and not first:
                    experts(i - 1, 1 - parity, 0)
                    experts(i - 1, 1 - parity, 1)
                if runs(i, 3):
                    combine(i - 3, 1 - parity)

            pe.wait_ge(s["logits_kept"], B)
            expert_steady(pe, expert_step)


def constants():
    import numpy as np
    half = RK // 2
    inv_freq = (1.0 / np.float32(10000.0) ** (np.arange(0, RK, 2, dtype=np.float32) / np.float32(RK))).astype(np.float32)
    angle = (np.arange(T, dtype=np.float32)[None, :] * inv_freq[:, None]).astype(np.float64)
    cos, sin = np.cos(angle), np.sin(angle)
    log_decay = np.log1p(-np.exp2(-5.0 - np.arange(RH)))[:, None, None] * np.arange(T)[None, None, :]
    cos_h = np.broadcast_to(np.concatenate([cos, cos])[None], (RH, RK, T))
    sin_h = np.broadcast_to(np.concatenate([sin, -sin])[None], (RH, RK, T))
    up, down = np.exp(log_decay) * RK ** -0.5, np.exp(-log_decay)
    c = {}
    c["cos_t"] = np.stack([cos_h * up, cos_h * down], axis=2).reshape(D, 2 * T).astype(np.float32)
    c["sin_t"] = np.stack([sin_h * up, sin_h * down], axis=2).reshape(D, 2 * T).astype(np.float32)
    c["causal"] = (np.arange(P)[:, None] <= np.arange(P)[None, :]).astype(np.float32)
    c["ident"] = np.eye(P, dtype=np.float32)
    c["head_mask"] = (np.arange(3 * GR)[:, None] % GR // XD == np.arange(GH)[None, :]).astype(np.float32)
    c["head_pick"] = (np.arange(2 * XH)[:, None] % XH == np.arange(XH * XK)[None, :] // XK).astype(np.float32).reshape(2 * XH, PAIRS, 2, XK)
    pick = np.zeros((D, 2, XG, 3, GR), np.float32)
    for third, part in enumerate((0, 1, 0)):
        pick[:, part, :, third, :] = np.eye(D, dtype=np.float32).reshape(D, XG, GR)
    c["row_pick"] = pick.reshape(D, 2, XG, 3 * GR)
    c["iota_e"] = np.broadcast_to(np.arange(E, dtype=np.float32), (P, E)).copy()
    return c


def kernel(x, ctx_1024, L0_attn_Wq, L0_attn_Wk, L0_attn_Wv, L0_attn_Wg, L0_attn_Wo, L0_attn_g_norm_w,
           L0_xattn_w_q, L0_xattn_w_k, L0_xattn_w_v, L0_xattn_w_o,
           L0_ffn_gate_w, L0_ffn_expert_w, L0_ffn_expert_b, L0_ffn_combine_w):
    import numpy as np
    import concourse.bacc as bacc
    from concourse.bass_utils import run_bass_kernel_spmd

    x = np.asarray(x)
    wq, wk = np.asarray(L0_attn_Wq), np.asarray(L0_attn_Wk)
    bias = np.zeros((64, E * D), np.float32)
    bias[0] = bias[32] = np.asarray(L0_ffn_expert_b).reshape(-1)
    arrays = constants()
    arrays["tables"] = np.stack([arrays.pop("cos_t"), arrays.pop("sin_t")], axis=1)
    arrays["squares"] = np.stack([arrays.pop("ident"), arrays.pop("causal")], axis=1)
    arrays["xT"] = x.reshape(B * T, D).T
    arrays["x"] = x.reshape(B, J, P, D).transpose(0, 2, 1, 3)
    arrays["w_qk"] = np.stack([wq.T, wk.T], axis=1)
    arrays["w_vg"] = np.stack([np.asarray(L0_attn_Wv).T, np.asarray(L0_attn_Wg).T], axis=1)
    arrays["w_ret_o"] = np.asarray(L0_attn_Wo).T.reshape(2, P, D).transpose(1, 0, 2)
    arrays["norm_w"] = np.tile(np.asarray(L0_attn_g_norm_w), P // RV).reshape(P, 1)
    arrays["w_x"] = np.stack([np.asarray(w).T for w in (L0_xattn_w_q, L0_xattn_w_v, L0_xattn_w_o)], axis=1)
    arrays["w_k3"] = np.repeat(np.asarray(L0_xattn_w_k).T.reshape(D, XG, 1, GR), 3, axis=2).reshape(D, XG, 3 * GR)
    context = np.asarray(ctx_1024).reshape(B * XK, D)
    arrays["ctxT"] = np.concatenate([context, context[:XK]]).T
    arrays["gate_w"] = np.asarray(L0_ffn_gate_w).T
    arrays["expert_w"] = np.asarray(L0_ffn_expert_w).transpose(2, 0, 1).reshape(D, E * D)
    arrays["bias"] = bias
    arrays["comb_w"] = np.asarray(L0_ffn_combine_w).T
    arrays = {n: np.ascontiguousarray(v) for n, v in arrays.items()}

    nc = bacc.Bacc("TRN2", target_bir_lowering=False, num_devices=1)
    ins = {n: nc.dram_tensor(n + "_dram", v.shape, mybir.dt.from_np(v.dtype), kind="ExternalInput").ap() for n, v in arrays.items()}
    out = nc.dram_tensor("out_dram", (B, P, J, D), F32, kind="ExternalOutput").ap()
    post_ln_decoder(nc, ins, out)
    r = run_bass_kernel_spmd(nc, [{n + "_dram": v for n, v in arrays.items()}], core_ids=[0])
    return r.results[0]["out_dram"].transpose(0, 2, 1, 3).reshape(B, T, D)
```
